# Optimizing a Trainium2 kernel written in Bass

```python
import numpy as np
import jax
import jax.numpy as jnp

def _softmax(x, axis=-1):
    return jax.nn.softmax(x, axis=axis)

def _gelu(x):
    return jax.nn.gelu(x, approximate=True)

def _silu(x):
    return jax.nn.silu(x)

def _sigmoid(x):
    return jax.nn.sigmoid(x)

def _layernorm(x, axis=-1, eps=1e-05):
    m = jnp.mean(x, axis=axis, keepdims=True)
    v = jnp.var(x, axis=axis, keepdims=True)
    return (x - m) / jnp.sqrt(v + eps)

def _scatter_add(tgt, idx, src, axis=0):
    return tgt.at[idx].add(src)

def _segment_sum(src, seg, n):
    return jax.ops.segment_sum(src, seg, n)
kernel_name = 'mk_decoder_preln_d1_seqx_r4_973a48'

def setup_inputs(seed: int=0):
    np.random.seed(seed)
    _w = jnp.asarray

    def _rec_inputs():
        import jax
        import jax.numpy as jnp
        _rk = jax.random.key(seed)
        x = -0.0002928 + 1 * jax.random.normal(jax.random.fold_in(_rk, 1), (8, 512, 256), jnp.float32)
        _lenS = 512 - jax.random.randint(jax.random.fold_in(_rk, 7), (8,), 0, max(1, 512 // 4) + 1, jnp.int32)
        _lenS2 = 512 - jax.random.randint(jax.random.fold_in(_rk, 8), (8,), 0, max(1, 512 // 4) + 1, jnp.int32)
        _ctx_1024P = jax.random.normal(jax.random.fold_in(_rk, 11), (8, 16, 256), jnp.float32)
        _ctx_1024c = jax.random.dirichlet(jax.random.fold_in(_rk, 511), 0.3 * jnp.ones((16,), jnp.float32), (8, 512))
        _ctx_1024t = jnp.einsum('bsk,bkd->bsd', _ctx_1024c, _ctx_1024P)
        _ctx_1024t = _ctx_1024t * jax.lax.rsqrt(jnp.mean(jnp.square(_ctx_1024t)) + 1e-12) * 0.953939
        ctx_1024 = -1.39393e-06 + 0.999914 * (_ctx_1024t + 0.3 * jax.random.normal(jax.random.fold_in(_rk, 611), (8, 512, 256), jnp.float32))
        return (x, ctx_1024)
    x, ctx_1024 = _rec_inputs()

    def _L0_attn_setup():
        import jax, jax.numpy as jnp
        import numpy as np
        B, L, D, ORDER = (2, 2048, 256, 2)
        HID = 64

        def _fft_conv(x, h):
            Ln = x.shape[-1]
            n = 2 * Ln
            xf = jnp.fft.rfft(x, n=n)
            hf = jnp.fft.rfft(h, n=n)
            return jnp.fft.irfft(xf * hf[None], n=n)[..., :Ln]
        key = jax.random.key(seed)
        ks = jax.random.split(key, 7)

        def w(k, shape, fan_in):
            return jax.random.normal(k, shape, jnp.float32) / np.float32(np.sqrt(fan_in))
        return {'x': jax.random.normal(ks[0], (B, L, D), jnp.float32), 'W_in': w(ks[1], ((ORDER + 1) * D, D), D), 'W_out': w(ks[2], (D, D), D), 'f_w1': w(ks[3], (ORDER, HID, 1), 1), 'f_b1': jnp.zeros((ORDER, HID), jnp.float32), 'f_w2': w(ks[4], (ORDER, D, HID), HID), 'f_b2': jnp.zeros((ORDER, D), jnp.float32)}
    _L0_attn_all = _L0_attn_setup()
    _L0_attn_in = {k: v for k, v in _L0_attn_all.items() if k in ('W_in', 'W_out', 'f_w1', 'f_b1', 'f_w2', 'f_b2')}
    del _L0_attn_all

    def _L0_xattn_setup():
        import jax, jax.numpy as jnp
        import numpy as np
        B, S, DIM, NH = (2, 512, 256, 8)
        DH = DIM // NH
        GATE_SOFT_CAP = 15.0
        BACKEND_EPS = 5e-05
        NORM_EPS = 1e-06

        def _mlstm_parallel(q, k, v, i_pre, f_pre):
            log_fg = jax.nn.log_sigmoid(f_pre)
            lf_cs = jnp.cumsum(log_fg, axis=-1)
            lf = jnp.concatenate([jnp.zeros_like(lf_cs[..., :1]), lf_cs], axis=-1)
            log_d = lf[..., 1:, None] - lf[..., None, 1:] + i_pre[..., None, :]
            t_idx = jnp.arange(q.shape[2])
            mask = t_idx[:, None] >= t_idx[None, :]
            log_d = jnp.where(mask, log_d, -jnp.inf)
            m = jnp.max(log_d, axis=-1, keepdims=True)
            d_mat = jnp.exp(log_d - m)
            scores = jnp.einsum('bhtd,bhsd->bhts', q, k) * (1.0 / np.sqrt(DH))
            s_mat = scores * d_mat
            denom = jnp.maximum(jnp.abs(jnp.sum(s_mat, axis=-1, keepdims=True)), jnp.exp(-m)) + BACKEND_EPS
            return jnp.einsum('bhts,bhsd->bhtd', s_mat, v) / denom
        key = jax.random.key(seed)
        kq, kk, kv, kw = jax.random.split(key, 4)
        q = jax.random.normal(kq, (B, S, DIM), dtype=jnp.float32)
        k = jax.random.normal(kk, (B, S, DIM), dtype=jnp.float32)
        v = jax.random.normal(kv, (B, S, DIM), dtype=jnp.float32)
        ifgate_w = 0.02 * jax.random.normal(kw, (2 * NH, 3 * DIM), dtype=jnp.float32)
        ifgate_b = jnp.concatenate([jnp.full((NH,), -10.0, dtype=jnp.float32), jnp.linspace(3.0, 6.0, NH, dtype=jnp.float32)])
        outnorm_w = jnp.zeros((DIM,), dtype=jnp.float32)
        return {'q': q, 'k': k, 'v': v, 'ifgate_w': ifgate_w, 'ifgate_b': ifgate_b, 'outnorm_w': outnorm_w}
    _L0_xattn_all = _L0_xattn_setup()
    _L0_xattn_in = {k: v for k, v in _L0_xattn_all.items() if k in ('ifgate_w', 'ifgate_b', 'outnorm_w')}
    del _L0_xattn_all

    def _L0_ffn_setup():
        import jax, jax.numpy as jnp
        import numpy as np
        EPS = 1e-05

        def _quantize(W):
            gamma = jnp.mean(jnp.abs(W))
            return jnp.clip(jnp.round(W / (gamma + EPS)), -1.0, 1.0)
        key = jax.random.key(seed)
        k_x, k_w1, k_b1, k_w2, k_b2 = jax.random.split(key, 5)
        n_embd = 256
        d_ff = 4 * n_embd
        B, S = (4, 1024)
        bound1 = 1.0 / np.sqrt(n_embd)
        bound2 = 1.0 / np.sqrt(d_ff)
        x = jax.random.normal(k_x, (B, S, n_embd), dtype=jnp.float32)
        W1 = jax.random.uniform(k_w1, (d_ff, n_embd), jnp.float32, -bound1, bound1)
        b1 = jax.random.uniform(k_b1, (d_ff,), jnp.float32, -bound1, bound1)
        W2 = jax.random.uniform(k_w2, (n_embd, d_ff), jnp.float32, -bound2, bound2)
        b2 = jax.random.uniform(k_b2, (n_embd,), jnp.float32, -bound2, bound2)
        return {'x': x, 'W1': W1, 'b1': b1, 'W2': W2, 'b2': b2}
    _L0_ffn_all = _L0_ffn_setup()
    _L0_ffn_in = {k: v for k, v in _L0_ffn_all.items() if k in ('W1', 'b1', 'W2', 'b2')}
    del _L0_ffn_all
    return {'x': x, 'ctx_1024': ctx_1024, 'L0_attn_W_in': _L0_attn_in['W_in'], 'L0_attn_W_out': _L0_attn_in['W_out'], 'L0_attn_f_w1': _L0_attn_in['f_w1'], 'L0_attn_f_b1': _L0_attn_in['f_b1'], 'L0_attn_f_w2': _L0_attn_in['f_w2'], 'L0_attn_f_b2': _L0_attn_in['f_b2'], 'L0_xattn_ifgate_w': _L0_xattn_in['ifgate_w'], 'L0_xattn_ifgate_b': _L0_xattn_in['ifgate_b'], 'L0_xattn_outnorm_w': _L0_xattn_in['outnorm_w'], 'L0_ffn_W1': _L0_ffn_in['W1'], 'L0_ffn_b1': _L0_ffn_in['b1'], 'L0_ffn_W2': _L0_ffn_in['W2'], 'L0_ffn_b2': _L0_ffn_in['b2']}

def reference(x, ctx_1024, L0_attn_W_in, L0_attn_W_out, L0_attn_f_w1, L0_attn_f_b1, L0_attn_f_w2, L0_attn_f_b2, L0_xattn_ifgate_w, L0_xattn_ifgate_b, L0_xattn_outnorm_w, L0_ffn_W1, L0_ffn_b1, L0_ffn_W2, L0_ffn_b2):
    import jax
    import jax.numpy as jnp

    def _L0_attn_ref(x, W_in, W_out, f_w1, f_b1, f_w2, f_b2):
        import jax, jax.numpy as jnp
        import numpy as np
        B, L, D, ORDER = (2, 2048, 256, 2)
        HID = 64

        def _fft_conv(x, h):
            Ln = x.shape[-1]
            n = 2 * Ln
            xf = jnp.fft.rfft(x, n=n)
            hf = jnp.fft.rfft(h, n=n)
            return jnp.fft.irfft(xf * hf[None], n=n)[..., :Ln]
        Bn, Ln, Dn = x.shape
        proj = x @ W_in.T
        splits = jnp.split(proj, ORDER + 1, axis=-1)
        v = jnp.swapaxes(splits[0], 1, 2)
        t = jnp.linspace(0.0, 1.0, Ln, dtype=x.dtype)[:, None]
        for i in range(ORDER):
            h = jax.nn.silu(t @ f_w1[i].T + f_b1[i]) @ f_w2[i].T + f_b2[i]
            v = _fft_conv(v, h.T)
            v = v * jnp.swapaxes(splits[i + 1], 1, 2)
        out = jnp.swapaxes(v, 1, 2)
        return out @ W_out.T

    def _L0_xattn_ref(q, k, v, ifgate_w, ifgate_b, outnorm_w):
        import jax, jax.numpy as jnp
        import numpy as np
        B, S, DIM, NH = (2, 512, 256, 8)
        DH = DIM // NH
        GATE_SOFT_CAP = 15.0
        BACKEND_EPS = 5e-05
        NORM_EPS = 1e-06

        def _mlstm_parallel(q, k, v, i_pre, f_pre):
            log_fg = jax.nn.log_sigmoid(f_pre)
            lf_cs = jnp.cumsum(log_fg, axis=-1)
            lf = jnp.concatenate([jnp.zeros_like(lf_cs[..., :1]), lf_cs], axis=-1)
            log_d = lf[..., 1:, None] - lf[..., None, 1:] + i_pre[..., None, :]
            t_idx = jnp.arange(q.shape[2])
            mask = t_idx[:, None] >= t_idx[None, :]
            log_d = jnp.where(mask, log_d, -jnp.inf)
            m = jnp.max(log_d, axis=-1, keepdims=True)
            d_mat = jnp.exp(log_d - m)
            scores = jnp.einsum('bhtd,bhsd->bhts', q, k) * (1.0 / np.sqrt(DH))
            s_mat = scores * d_mat
            denom = jnp.maximum(jnp.abs(jnp.sum(s_mat, axis=-1, keepdims=True)), jnp.exp(-m)) + BACKEND_EPS
            return jnp.einsum('bhts,bhsd->bhtd', s_mat, v) / denom
        b, s, dim = q.shape
        gate_in = jnp.concatenate([q, k, v], axis=-1)
        pre = gate_in @ ifgate_w.T + ifgate_b
        pre = GATE_SOFT_CAP * jnp.tanh(pre / GATE_SOFT_CAP)
        i_pre = pre[..., :NH].transpose(0, 2, 1)
        f_pre = pre[..., NH:].transpose(0, 2, 1)
        qh = q.reshape(b, s, NH, DH).transpose(0, 2, 1, 3)
        kh = k.reshape(b, s, NH, DH).transpose(0, 2, 1, 3)
        vh = v.reshape(b, s, NH, DH).transpose(0, 2, 1, 3)
        h = _mlstm_parallel(qh, kh, vh, i_pre, f_pre)
        rrms = jax.lax.rsqrt(jnp.mean(h * h, axis=-1, keepdims=True) + NORM_EPS)
        gain = (1.0 + outnorm_w).reshape(1, NH, 1, DH)
        h = h * rrms * gain
        return h.transpose(0, 2, 1, 3).reshape(b, s, dim)

    def _L0_ffn_ref(x, W1, b1, W2, b2):
        import jax, jax.numpy as jnp
        import numpy as np
        EPS = 1e-05

        def _quantize(W):
            gamma = jnp.mean(jnp.abs(W))
            return jnp.clip(jnp.round(W / (gamma + EPS)), -1.0, 1.0)
        Wq1 = _quantize(W1)
        Wq2 = _quantize(W2)
        h = jax.nn.relu(jnp.einsum('bsd,fd->bsf', x, Wq1) + b1)
        out = jnp.einsum('bsf,df->bsd', h, Wq2) + b2
        return out
    x = x + _L0_attn_ref(_layernorm(x, axis=-1), L0_attn_W_in, L0_attn_W_out, L0_attn_f_w1, L0_attn_f_b1, L0_attn_f_w2, L0_attn_f_b2)
    x = x + _L0_xattn_ref(_layernorm(x, axis=-1), ctx_1024, ctx_1024, L0_xattn_ifgate_w, L0_xattn_ifgate_b, L0_xattn_outnorm_w)
    x = x + _L0_ffn_ref(_layernorm(x, axis=-1), L0_ffn_W1, L0_ffn_b1, L0_ffn_W2, L0_ffn_b2)
    return x

_drawn_inputs = setup_inputs


def setup_inputs(seed=0):
    import zlib

    import numpy as np

    out = dict(_drawn_inputs(seed))
    spreads = {'L0_attn_f_b1': (0.0, 0.1), 'L0_attn_f_b2': (0.0, 0.1), 'L0_xattn_outnorm_w': (0.0, 0.299)}
    factors = {'L0_ffn_b1': 21.867, 'L0_ffn_b2': 64.0}
    for name, (base, spread) in spreads.items():
        noise = np.random.default_rng([zlib.crc32(name.encode()), seed]).standard_normal(out[name].shape)
        drawn = base * np.exp(spread * noise) if base else spread * noise
        out[name] = jnp.asarray(drawn.astype(out[name].dtype))
    for name, factor in factors.items():
        out[name] = (out[name] * factor).astype(out[name].dtype)
    return out
```

```python
from contextlib import ExitStack

import numpy as np

from concourse.bass import ds
from concourse import mybir

F32 = mybir.dt.float32
F32R = mybir.dt.float32r
I32 = mybir.dt.int32
BF16 = mybir.dt.bfloat16
ALU = mybir.AluOpType
ACT = mybir.ActivationFunctionType
AX_X = mybir.AxisListType.X

P = 128
B, L, D = 8, 512, 256
NT = L // P
KT = D // P
TILES = B * NT
PB = 2
STEPS = B // PB
NC = PB * D
HALF = L // 2
ORDER, HID = 2, 64
NFFT = 2 * L
FJ = 4
LN_EPS = 1e-5

NH, DH = 8, 32
BH = B * NH
CAP = 15.0
DEN_EPS, RMS_EPS = 5e-5, 1e-6
V1 = DH + 1
PADH = 2
NPART = 3
NEG = -1e30

FF = 1024
FT = FF // P
Q_EPS = 1e-5
ROUND = 1.5 * 2.0**23


def transform_tables():
    slot = np.arange(FJ * P)
    even = slot < HALF
    k = np.where(even, 2 * slot, 2 * (slot - HALF) + 1).astype(np.float64)
    k_sin = k.copy()
    k_sin[0] = NFFT // 2
    n = np.arange(HALF) + 0.5
    cos = np.cos(2 * np.pi / NFFT * np.outer(n, k))
    sin = np.sin(2 * np.pi / NFFT * np.outer(n, k_sin))
    both = np.stack([cos.reshape(HALF, FJ, P), sin.reshape(HALF, FJ, P)], axis=2)
    fwd = both.reshape(HALF // P, P, FJ, 2, P).transpose(1, 0, 2, 3, 4)
    w = np.full(FJ * P, 2.0 / NFFT)
    w[0] = 1.0 / NFFT
    inv = (both * w.reshape(1, FJ, 1, P)).transpose(3, 1, 2, 0)
    m = np.arange(L)
    hc = np.cos(2 * np.pi / NFFT * np.outer(m, k))
    hs = np.sin(2 * np.pi / NFFT * np.outer(m, k))
    hs[:, 0] = 0.0
    hc_sin = np.cos(2 * np.pi / NFFT * np.outer(m, k_sin[:P]))
    filt = np.concatenate([hc, hs, hc_sin], axis=1)
    filt_t = filt.reshape(NT, P, -1).transpose(1, 0, 2)
    f = lambda a: np.ascontiguousarray(a, dtype=np.float32)
    return f(fwd), f(inv), f(filt_t), f(filt.sum(0)[None, :])


def attention_tables():
    s, t = np.arange(P)[:, None], np.arange(P)[None, :]
    mask = np.tile(np.where(s <= t, 0.0, NEG), (1, NT)).astype(np.float32)
    chunk = np.zeros((NPART, NT, NH, NT, P), np.float32)
    for c in range(NT):
        chunk[:, c, :, c, :] = 1.0
    return mask, chunk.reshape(NPART * NT, NH * NT * P)


def tables():
    fwd, inv, filt, fsum = transform_tables()
    mask, chunk = attention_tables()
    time = np.ascontiguousarray(np.linspace(0.0, 1.0, L, dtype=np.float32).reshape(NT, P).T)
    head = np.arange(P)[:, None] // DH == np.arange(NH // KT * V1)[None, :] // V1
    heads = (head / np.sqrt(DH)).astype(np.float32)
    return {"fwd": fwd, "inv": inv, "filt": filt, "fsum": fsum, "time": time, "mask": mask, "chunk": chunk,
            "heads": heads}


class Count:

    def __init__(self, eng, sem):
        self.eng, self.sem, self.base, self.n = eng, sem, 0, 0

    def from_(self, base):
        self.base, self.n = base, 0

    def then(self, ins):
        self.n += 1
        ins.then_inc(self.sem, 1)
        self.eng.wait_ge(self.sem, self.base + self.n)


def inverse_root(own, dve, y, v, t):
    own.then(dve.tensor_scalar(y.bitcast(I32), v.bitcast(I32), -0.5, float(0x5F3759DF), ALU.mult, ALU.add))
    for _ in range(3):
        own.then(dve.tensor_tensor(t, y, y, ALU.mult))
        own.then(dve.scalar_tensor_tensor(t, t, -0.5, v, ALU.mult, ALU.mult))
        own.then(dve.scalar_tensor_tensor(y, t, 1.5, y, ALU.add, ALU.mult))


def decoder_layer(nc, x, ctx, w_in, w_out, f_w1, f_b1, f_w2, f_b2, ifw, ifb, onw, w1, b1, w2, b2,
                  c_fwd, c_inv, c_filt, c_fsum, c_time, c_mask, c_chunk, c_heads, out):
    NS = 2 * FJ + 1
    FC = NS * P
    HV = NH * V1
    GV = HV // KT
    PAIRS = (NT - 1) * NT // 2
    NEN = PAIRS + (NT - 1) + NT

    main = ExitStack()
    with main:
        def put(stack, name, shape, dt=F32):
            return stack.enter_context(nc.sbuf_tensor(name, shape, dt))

        def sem(name):
            return main.enter_context(nc.semaphore(name))

        def sb(name, shape, dt=F32):
            return put(main, name, shape, dt)

        bank = [main.enter_context(nc.psum_tensor(f"bank{i}", [P, 512], F32)) for i in range(8)]
        scr_q = nc.dram_tensor("scr_q", [B, P, KT * L], F32, kind="Internal").ap()
        scr_k = nc.dram_tensor("scr_k", [B, P, KT * L], F32, kind="Internal").ap()
        scr_a = nc.dram_tensor("scr_a", [NPART, NT, BH, P], BF16, kind="Internal").ap()
        scr_m = nc.dram_tensor("scr_m", [NPART, BH, L], BF16, kind="Internal").ap()

        res = sb("res", [P, TILES, D])
        ident = sb("ident", [P, P])
        mv = sb("mv", [P, TILES, 2])
        stats = sb("stats", [P, TILES, 6])
        rstd = sb("rstd", [P, TILES])
        var_eps = sb("var_eps", [P, TILES])
        nwt = sb("nwt", [P, TILES])
        win_t = sb("win_t", [P, KT, 3 * D])
        wout_t = sb("wout_t", [P, KT, D])
        wg_t = sb("wg_t", [P, 6, 2 * NH])
        wq1_t = sb("wq1_t", [P, KT, FF], F32R)
        wq2_t = sb("wq2_t", [P, FT, D], F32R)
        b1_col = sb("b1_col", [P, FT])
        b2_bc = sb("b2_bc", [P, D])
        gain = sb("gain", [P, D])
        gates = sb("gates", [P, NT, 2, B, NH])

        pa = ExitStack()
        fwd = put(pa, "fwd", [P, 2, FJ, 2, P])
        inv = put(pa, "inv", [P, FJ, 2, HALF])
        filt = put(pa, "filt", [P, ORDER, NS, D])
        pw = ExitStack()
        w_nat = put(pw, "w_nat", [P, 6, D])
        wo_nat = put(pw, "wo_nat", [P, KT, D])
        g_nat = put(pw, "g_nat", [2 * NH, 3 * D])
        f2_nat = put(pw, "f2_nat", [P, KT, ORDER, HID])
        f2_z = put(pw, "f2_z", [P, ORDER, D])
        fw1_bc = put(pw, "fw1_bc", [P, ORDER * HID])
        fb1_bc = put(pw, "fb1_bc", [P, ORDER * HID])
        fb2 = put(pw, "fb2", [P, ORDER, D])
        feat = put(pw, "feat", [P, NT, P])
        fs_t = put(pw, "fs_t", [P, FC])
        h_fwd = put(pw, "h_fwd", [P, NT, FC])
        fsum = put(pw, "fsum", [P, FC])
        time = put(pw, "time", [P, NT])
        w1_nat = put(pw, "w1_nat", [P, FT, D])
        w2_nat = put(pw, "w2_nat", [P, KT, FF])
        qsum = put(pw, "qsum", [P, 2])
        qden = put(pw, "qden", [P, 2])
        qrec = put(pw, "qrec", [P, 2])
        ones = put(pw, "ones", [P, P])
        pw.close()
        xn = put(pa, "xn", [P, PB * NT, D])
        xn_t = put(pa, "xn_t", [P, KT, PB, L])
        xf = put(pa, "xf", [P, 2, KT, PB, HALF])
        vf = put(pa, "vf", [P, 2, 2, NC])
        g1 = put(pa, "g1", [P, 2, 2, NC])
        v2_t = g1[:].rearrange("p a b (c d) -> p (a b c d)", c=PB).rearrange("p (b k t) -> p b k t", b=PB, k=KT)
        g2_t = put(pa, "g2_t", [P, PB, KT, L])
        prod = put(pa, "prod", [P, 2, 4, NC])
        spec = put(pa, "spec", [P, 2, 2, NC])
        even = put(pa, "even", [P, 2, NC])
        even_q = even[:].rearrange("p a (b n) -> p (a b) n", b=PB)
        ysum = put(pa, "ysum", [P, 2, 2, NC])
        ysum_q = ysum[:].rearrange("p a b (c n) -> p (a b c) n", c=PB).rearrange("p (q s) n -> p q s n", s=2)
        pa.close()

        pb = ExitStack()
        ctx_s = put(pb, "ctx_s", [P, 2, NT, D])
        q_t = put(pb, "q_t", [P, 2, KT, L])
        k_t = put(pb, "k_t", [P, 2, KT, L])
        mask = put(pb, "mask", [P, L], BF16)
        identb = put(pb, "identb", [P, P], BF16)
        heads = put(pb, "heads", [P, GV])
        en = put(pb, "en", [P, NEN, BH])
        a_st = put(pb, "a_st", [NPART * NT + NPART, 2, NH, P], BF16)
        m_mv = put(pb, "m_mv", [NPART * NT + NPART, 2, NH, L], BF16)
        pg = ExitStack()
        qn = put(pg, "qn", [P, 2, NT, D])
        wkv = put(pg, "wkv", [P, KT, 2 * NH])
        bg = put(pg, "bg", [BH, 2])
        th = put(pg, "th", [BH, 2, L])
        sg = put(pg, "sg", [BH, 6, L])
        lf = put(pg, "lf", [BH, L])
        aw = put(pg, "aw", [BH, L])
        mx = put(pg, "mx", [BH, L])
        nmx = put(pg, "nmx", [BH, L])
        msum = put(pg, "msum", [BH, L])
        ek = put(pg, "ek", [BH, NEN, P])
        ap3 = put(pg, "ap3", [BH, NPART, L], BF16)
        mp3 = put(pg, "mp3", [BH, NPART, L], BF16)
        rem = put(pg, "rem", [BH, 4, L])
        onesrow = put(pg, "onesrow", [BH, L])
        pg.close()
        cv = put(pb, "cv", [P, 2, NT, NH + PADH, V1])
        edec = put(pb, "edec", [P, 2, L])
        pmat = put(pb, "pmat", [P, 2, L])
        vs = put(pb, "vs", [P, PAIRS, NH, V1])
        bd = put(pb, "bd", [P, KT, NT - 1, GV])
        inter = put(pb, "inter", [P, NT - 1, NH, V1])
        num = put(pb, "num", [P, 2, NT, NH, V1])
        sq = put(pb, "sq", [P, NT, NH, DH])
        hout = put(pb, "hout", [P, NT, NH, DH])
        tiny = put(pb, "tiny", [P, 8, NT, NH])
        pb.close()

        pc = ExitStack()
        x3 = put(pc, "x3", [P, 2, NT, D])
        x3h = put(pc, "x3h", [P, 2, KT, L], F32R)
        x3l = put(pc, "x3l", [P, 2, KT, L], F32R)
        ff = put(pc, "ff", [P, 3, L])
        ffh = put(pc, "ffh", [P, 4, L], F32R)
        ffl = put(pc, "ffl", [P, 4, L], F32R)
        rb = put(pc, "rb", [P, 2, NT, D])
        ob = put(pc, "ob", [P, 2, NT, D])
        pc.close()

        s_ldf = sem("s_ldf")
        s_ldx = sem("s_ldx")
        s_ldt = sem("s_ldt")
        s_ldw = sem("s_ldw")
        s_ldq = sem("s_ldq")
        s_zero = sem("s_zero")
        s_feat = sem("s_feat")
        s_silu = sem("s_silu")
        s_prep = sem("s_prep")
        s_prepc = sem("s_prepc")
        s_qabs = sem("s_qabs")
        s_quant = sem("s_quant")
        own_p = sem("own_p")
        s_xn = sem("s_xn")
        s_tp = sem("s_tp")
        s_xt = sem("s_xt")
        s_xf = sem("s_xf")
        s_vp = sem("s_vp")
        s_vf = sem("s_vf")
        s_gp = sem("s_gp")
        s_g1 = sem("s_g1")
        s_hp = sem("s_hp")
        s_g2 = sem("s_g2")
        s_x = sem("s_x")
        s_xu = sem("s_xu")
        s_y = sem("s_y")
        s_yu = sem("s_yu")
        s_ev1 = sem("s_ev1")
        s_u = sem("s_u")
        own_a = sem("own_a")
        s_v1 = sem("s_v1")
        s_ev2 = sem("s_ev2")
        s_u2 = sem("s_u2")
        s_v2 = sem("s_v2")
        s_op = sem("s_op")
        s_res = sem("s_res")
        s_out = sem("s_out")
        s_st2 = sem("s_st2")
        own_n = sem("own_n")
        s_cl = [sem(f"s_cl{u}") for u in range(2)]
        s_qn = sem("s_qn")
        s_gt = sem("s_gt")
        s_gx = sem("s_gx")
        s_gg = sem("s_gg")
        s_gv = sem("s_gv")
        s_sq = [sem(f"s_sq{u}") for u in range(2)]
        s_bgl = sem("s_bgl")
        s_bg = sem("s_bg")
        s_one = sem("s_one")
        s_rows = sem("s_rows")
        s_tanh = sem("s_tanh")
        s_absf = sem("s_absf")
        s_expf = sem("s_expf")
        s_onep = sem("s_onep")
        s_lnp = sem("s_lnp")
        s_aw = sem("s_aw")
        s_mx = sem("s_mx")
        s_ms = sem("s_ms")
        s_ek = sem("s_ek")
        s_ent = sem("s_ent")
        s_en = sem("s_en")
        s_parts = sem("s_parts")
        s_scr = sem("s_scr")
        s_lda = sem("s_lda")
        s_ldm = sem("s_ldm")
        s_idb = sem("s_idb")
        own_s = sem("own_s")
        s_bl = [sem(f"s_bl{u}") for u in range(2)]
        s_cv = sem("s_cv")
        s_vs = sem("s_vs")
        s_sp = sem("s_sp")
        s_bd = sem("s_bd")
        s_ip = sem("s_ip")
        s_in = sem("s_in")
        s_sc = sem("s_sc")
        s_ed = sem("s_ed")
        s_pm = sem("s_pm")
        s_pv = sem("s_pv")
        s_n0 = sem("s_n0")
        s_num = sem("s_num")
        s_sqr = sem("s_sqr")
        s_ra = sem("s_ra")
        s_st3 = sem("s_st3")
        own_b = sem("own_b")
        s_oned = sem("s_oned")
        own_f = sem("own_f")
        own_c = sem("own_c")
        s_x3 = sem("s_x3")
        s_xp = sem("s_xp")
        s_xh = sem("s_xh")
        s_xl = sem("s_xl")
        s_fp = sem("s_fp")
        s_fr = sem("s_fr")
        s_fh = sem("s_fh")
        s_fl = sem("s_fl")
        s_fo = sem("s_fo")
        s_rb = sem("s_rb")
        s_ob = sem("s_ob")
        s_so = [sem(f"s_so{u}") for u in range(2)]
        N_LDF, N_LDW, N_LDQ = 8, 3, 5
        WIN_JOBS, FS_COLS = 3, [(0, 512), (512, 1024), (1024, FC)]
        J_WOUT = WIN_JOBS
        J_GATE = J_WOUT + 1
        J_F2 = J_GATE + 1
        J_FS = J_F2 + 1
        J_H = J_FS + len(FS_COLS)
        J_SUM = J_H + NS
        J_W1 = J_SUM + 1
        J_W2 = J_W1 + FT // 2
        JOBS = J_W2 + FT // 2

        def copies(job):
            return job + 1 - (job >= J_SUM)

        block = main.enter_context(nc.Block())

        @block.sync
        def _(sp):
            for s in (*s_so, *s_sq):
                sp.sem_inc(s, 1)
            sp.dma_start(fw1_bc[:], f_w1.rearrange("o h a -> (o h a)").partition_broadcast(P)).then_inc(s_ldf, 16)
            sp.dma_start(fb1_bc[:], f_b1.rearrange("o h -> (o h)").partition_broadcast(P)).then_inc(s_ldf, 16)
            sp.dma_start(time[:], c_time).then_inc(s_ldf, 16)
            sp.dma_start(w_nat[:], w_in.rearrange("(i p) c -> p i c", p=P)).then_inc(s_ldw, 16)
            sp.dma_start(wo_nat[:], w_out.rearrange("(i p) c -> p i c", p=P)).then_inc(s_ldw, 16)
            sp.dma_start(g_nat[:], ifw).then_inc(s_ldw, 16)
            for o in range(ORDER):
                sp.dma_start(f2_nat[:, :, o], f_w2[o].rearrange("(k p) h -> p k h", p=P)).then_inc(s_ldf, 16)
            sp.wait_ge(s_zero, 6)
            sp.dma_start(fb2[0:1], f_b2.rearrange("(a o) d -> a o d", a=1)).then_inc(s_ldf, 16)
            sp.dma_start(fsum[0:1, :], c_fsum).then_inc(s_ldf, 16)
            sp.dma_start(h_fwd[:], c_filt).then_inc(s_ldf, 16)
            for b in range(B):
                sp.dma_start(res[:, b * NT:(b + 1) * NT, :], x[b].rearrange("(t p) d -> p t d", p=P)).then_inc(s_ldx, 16)
            sp.dma_start(fwd[:], c_fwd).then_inc(s_ldt, 16)
            sp.dma_start(inv[:], c_inv).then_inc(s_ldt, 16)
            sp.dma_start(w1_nat[:], w1.rearrange("(i p) c -> p i c", p=P)).then_inc(s_ldq, 16)
            sp.dma_start(w2_nat[:], w2.rearrange("(i p) c -> p i c", p=P)).then_inc(s_ldq, 16)
            sp.dma_start(b1_col[:], b1.rearrange("(i p) -> p i", p=P), allow_slow_non_contiguous=True).then_inc(s_ldq, 16)
            sp.dma_start(b2_bc[:], b2.partition_broadcast(P)).then_inc(s_ldq, 16)
            sp.dma_start(gain[:], onw.partition_broadcast(P)).then_inc(s_ldq, 16)
            sp.wait_ge(s_st2, STEPS)
            for b in range(B):
                for i in range(2):
                    sp.dma_start(bg[b * NH:(b + 1) * NH, i:i + 1], ifb.rearrange("(i h a) -> i h a", i=2, a=1)[i]).then_inc(s_bgl, 16)
            sp.dma_start(heads[:], c_heads).then_inc(s_lda, 16)

            def load_ctx(b, u, signal):
                sp.dma_start(ctx_s[:, u], ctx[ds(b, 1)].rearrange("a (t p) d -> p (a t) d", p=P)).then_inc(signal, 16)

            def store_qk(b, u):
                sp.dma_start(scr_q[ds(b, 1)].rearrange("a p (k t) -> p (a k) t", k=KT), q_t[:, u]).then_inc(s_sq[u], 16)
                sp.dma_start(scr_k[ds(b, 1)].rearrange("a p (k t) -> p (a k) t", k=KT), k_t[:, u]).then_inc(s_sq[u], 16)

            for u in range(2):
                load_ctx(u, u, s_cl[u])
            with sp.Fori(0, B // 2 - 1) as it:
                for u in range(2):
                    sp.wait_ge(s_gt, 1 + it * 8 + 4 * u + 4)
                    load_ctx(it * 2 + 2 + u, u, s_cl[u])
                    sp.wait_ge(s_gx, 1 + it * 8 + 4 * u + 4)
                    store_qk(it * 2 + u, u)
            for u in range(2):
                sp.wait_ge(s_gx, 1 + 4 * (B - 2 + u) + 4)
                store_qk(B - 2 + u, u)
            sp.wait_ge(s_parts, 2)
            for i in range(NPART):
                sp.dma_start(scr_a[i].rearrange("c h s -> h c s"), ap3[:, i].rearrange("h (c s) -> h c s", c=NT)).then_inc(s_scr, 16)
                sp.dma_start(scr_m[i], mp3[:, i]).then_inc(s_scr, 16)
            sp.wait_ge(s_scr, 16 * 2 * NPART)
            sp.wait_ge(s_one, 2)
            for u in range(2):
                sp.wait_ge(s_sq[u], 1 + 32 * (B // 2))
                sp.wait_ge(s_gt, 1 + 4 * B)

            def load_batch(b, u):
                load_ctx(b, u, s_bl[u])
                sp.dma_start(q_t[:, u], scr_q[ds(b, 1)].rearrange("a p (k t) -> p (a k) t", k=KT)).then_inc(s_bl[u], 16)
                sp.dma_start(k_t[:, u], scr_k[ds(b, 1)].rearrange("a p (k t) -> p (a k) t", k=KT)).then_inc(s_bl[u], 16)
                sp.dma_start(a_st[0:NPART * NT, u], scr_a.rearrange("i c h s -> (i c) h s")[:, ds(b * NH, NH)]).then_inc(s_bl[u], 16)
                sp.dma_start(m_mv[NPART * NT:NPART * NT + NPART, u], scr_m[:, ds(b * NH, NH)]).then_inc(s_bl[u], 16)

            for u in range(2):
                load_batch(u, u)
            with sp.Fori(0, B // 2 - 1) as it:
                for u in range(2):
                    sp.wait_ge(s_pv, 1 + it * (2 * NH) + (u + 1) * NH)
                    load_batch(it * 2 + 2 + u, u)
            with sp.Fori(0, B // 2) as it:
                for u in range(2):
                    sp.wait_ge(s_ob, 1 + it * 4 + 2 * u + 2)
                    sp.dma_start(out[ds(it * 2 + u, 1)].rearrange("a (t p) d -> p (a t) d", p=P), ob[:, u]).then_inc(s_so[u], 16)
            for u in range(2):
                sp.wait_ge(s_so[u], 1 + 16 * (B // 2))

        @block.gpsimd
        def _(pool):
            for s in (s_y, s_vs):
                pool.sem_inc(s, 1)
            pool.memset(ident[:], 0.0).then_inc(s_zero, 1)
            pool.memset(ones[:], 1.0).then_inc(s_zero, 1)
            pool.memset(f2_z[:], 0.0).then_inc(s_zero, 1)
            pool.memset(fsum[:], 0.0).then_inc(s_zero, 1)
            pool.memset(fb2[:], 0.0).then_inc(s_zero, 1)
            pool.wait_ge(s_zero, 5)
            pool.affine_select(out=ident[:], in_=ident[:], compare_op=ALU.not_equal, fill=1.0, base=0,
                               pattern=[[-1, P]], channel_multiplier=1).then_inc(s_zero, 1)
            with pool.Fori(0, STEPS) as it:
                for g in range(ORDER * FJ):
                    base = it * (ORDER * FJ) + g
                    pool.wait_ge(s_xu, base + 1)
                    pool.wait_ge(s_yu, 1 + (base - 1 if g else it * (ORDER * FJ)))
                    m = prod[:, g % 2]
                    pool.tensor_tensor(spec[:, g % 2, 0], m[:, 0], m[:, 1], ALU.subtract)
                    pool.tensor_tensor(spec[:, g % 2, 1], m[:, 2], m[:, 3], ALU.add).then_inc(s_y, 1)
            pool.wait_ge(s_st2, STEPS)
            pool.memset(onesrow[:], 1.0).then_inc(s_one, 1)
            pool.memset(a_st[:], 1.0).then_inc(s_one, 1)
            pool.dma_start(mask[:], c_mask).then_inc(s_ldm, 16)
            for u in range(2):
                pool.dma_start(m_mv[0:NPART * NT, u], c_chunk.rearrange("r (h t) -> r h t", h=NH)).then_inc(s_ldm, 16)
            pool.wait_ge(s_scr, 16 * 2 * NPART)
            pool.wait_ge(s_en, 2)
            pool.memset(cv[:, :, :, 0:NH, DH:V1], 1.0)
            pool.memset(cv[:, :, :, NH:NH + PADH], 0.0).then_inc(s_oned, 1)
            with pool.Fori(0, B // 2) as it:
                for u in range(2):
                    b = it * 2 + u
                    pool.wait_ge(s_cv, b + 1)
                    pool.wait_ge(s_sp, 1 + it * 4 + 2 * u)
                    for c in range(NT - 1):
                        i0 = c * (c + 1) // 2
                        w = en[:, i0:i0 + c + 1, ds(b * NH, NH)].unsqueeze(3).to_broadcast([P, c + 1, NH, V1])
                        last = pool.tensor_tensor(vs[:, i0:i0 + c + 1], cv[:, u, 0:c + 1, 0:NH], w, ALU.mult)
                    last.then_inc(s_vs, 1)
            pool.wait_ge(s_st3, B)
            with pool.Fori(0, B // 2) as it:
                for u in range(2):
                    pool.wait_ge(s_ob, 1 + it * 4)
                    pool.tensor_tensor(rb[:, u], res[:, ds(it * (2 * NT) + u * NT, NT)],
                                       b2_bc[:].unsqueeze(1).to_broadcast([P, NT, D]), ALU.add).then_inc(s_rb, 1)

        @block.scalar
        def _(act):
            for s in (s_xt, s_gx, s_n0, s_fr):
                act.sem_inc(s, 1)
            act.wait_ge(s_feat, NT)
            act.activation(feat[:], feat[:], ACT.Silu).then_inc(s_silu, 1)

            def copy_out(job, dst, src):
                act.wait_ge(s_prep, job + 1)
                act.activation(dst, src, ACT.Copy).then_inc(s_prepc, 1)

            for i in range(WIN_JOBS):
                copy_out(i, win_t[:, :, 2 * P * i:2 * P * (i + 1)], bank[i][:].rearrange("p (k n) -> p k n", k=KT))
            copy_out(J_WOUT, wout_t[:], bank[J_WOUT % 8][:].rearrange("p (k n) -> p k n", k=KT))
            copy_out(J_GATE, wg_t[:], bank[J_GATE % 8][:, 0:6 * 2 * NH].rearrange("p (k n) -> p k n", k=6))
            act.wait_ge(s_prep, J_F2 + 1)
            act.wait_ge(s_zero, 5)
            act.activation(f2_z[0:HID, 0], bank[J_F2 % 8][0:HID, 0:D], ACT.Copy)
            act.activation(f2_z[HID:P, 1], bank[J_F2 % 8][HID:P, 0:D], ACT.Copy).then_inc(s_prepc, 1)
            for i, (c0, c1) in enumerate(FS_COLS):
                copy_out(J_FS + i, fs_t[:, c0:c1], bank[(J_FS + i) % 8][:, 0:c1 - c0])
            for n in range(NS):
                copy_out(J_H + n, filt[:, :, n, :], bank[(J_H + n) % 8][:].rearrange("p (o n) -> p o n", o=ORDER))
            for i in range(FT // 2):
                copy_out(J_W1 + i, wq1_t[:, :, 2 * P * i:2 * P * (i + 1)],
                         bank[(J_W1 + i) % 8][:].rearrange("p (k n) -> p k n", k=KT))
            for i in range(FT // 2):
                copy_out(J_W2 + i, wq2_t[:, 2 * i:2 * i + 2, :],
                         bank[(J_W2 + i) % 8][:].rearrange("p (k n) -> p k n", k=KT))
            act.wait_ge(s_quant, 2)

            with act.Fori(0, STEPS) as it:
                for q in range(4):
                    act.wait_ge(s_tp, 1 + it * 4 + q + 1)
                    act.wait_ge(s_hp, 1 + it * 4)
                    act.wait_ge(s_xf, 1 + it * 2)
                    act.activation(xn_t[:, q % KT, q // KT, 0:HALF], bank[q][:, 0:HALF], ACT.Copy)
                    act.activation(xn_t[:, q % KT, q // KT, HALF:L], bank[q][:, L - 1:HALF - 1:-1],
                                   ACT.Copy).then_inc(s_xt, 1)
                for q in range(4):
                    act.wait_ge(s_vp, 1 + it * 4 + q + 1)
                    act.wait_ge(s_x, 1 + it * (ORDER * FJ))
                    act.activation(vf[:, q // 2, q % 2], bank[4 + q][:], ACT.Copy).then_inc(s_vf, 1)
                for q in range(4):
                    act.wait_ge(s_gp, it * 4 + q + 1)
                    act.wait_ge(s_op, 1 + it * 4)
                    act.activation(g1[:, q // 2, q % 2], bank[q][:], ACT.Copy).then_inc(s_g1, 1)
                for q in range(4):
                    act.wait_ge(s_hp, 1 + it * 4 + q + 1)
                    act.wait_ge(s_v2, 1 + it * 4)
                    act.activation(g2_t[:, q // KT, q % KT], bank[4 + q][:], ACT.Copy).then_inc(s_g2, 1)
                for nt in range(2):
                    act.wait_ge(s_yu, 1 + it * (ORDER * FJ) + FJ)
                    act.activation(even[:, nt], bank[4 + nt][:], ACT.Copy).then_inc(s_ev1, 1)
                for q in range(4):
                    act.wait_ge(s_yu, 1 + it * (ORDER * FJ) + 2 * FJ)
                    act.wait_ge(s_u, it * 2 + 2)
                    act.activation(even_q[:, q], bank[4 + q][:, 0:HALF], ACT.Copy).then_inc(s_ev2, 1)
            act.activation(identb[:], ident[:], ACT.Copy).then_inc(s_idb, 1)
            with act.Fori(0, B // 2) as it:
                for u in range(2):
                    act.wait_ge(s_sq[u], 1 + it * 32)
                    act.wait_ge(s_gg, 1 + it * 2)
                    for q in range(4):
                        act.wait_ge(s_gt, 1 + it * 8 + 4 * u + q + 1)
                        dst = (q_t if q < KT else k_t)[:, u, q % KT]
                        act.activation(dst, bank[4 * u + q][:], ACT.Copy).then_inc(s_gx, 1)
            act.wait_ge(s_bg, 1)
            act.wait_ge(s_rows, 2)
            for i in range(2):
                act.activation(th[:, i], bank[i][0:BH, :], ACT.Tanh, bias=bg[:, i:i + 1], scale=1.0 / CAP).then_inc(s_tanh, 1)
            act.wait_ge(s_absf, 1)
            act.activation(sg[:, 1], sg[:, 0], ACT.Exp, scale=-1.0).then_inc(s_expf, 1)
            act.wait_ge(s_onep, 1)
            act.activation(sg[:, 3], sg[:, 2], ACT.Ln).then_inc(s_lnp, 1)
            act.wait_ge(s_mx, 1)
            for c in range(NT - 1):
                i0 = c * (c + 1) // 2
                act.activation(ek[:, i0:i0 + c + 1].rearrange("h c s -> h (c s)"), aw[:, 0:(c + 1) * P], ACT.Exp,
                               bias=nmx[:, (c + 1) * P - 1:(c + 1) * P])
            for c in range(1, NT):
                act.activation(ek[:, PAIRS + c - 1], mx[:, c * P:(c + 1) * P], ACT.Exp, scale=-1.0, bias=mx[:, c * P - 1:c * P])
            act.wait_ge(s_ms, 1)
            act.activation(ek[:, PAIRS + NT - 1:NEN].rearrange("h c s -> h (c s)"), msum[:], ACT.Exp, scale=-1.0).then_inc(s_ek, 1)
            for i, (n0, n1) in enumerate(((0, 8), (8, NEN))):
                act.wait_ge(s_ent, i + 1)
                act.activation(en[:, n0:n1], bank[2 + i][:, 0:(n1 - n0) * BH].rearrange("p (n r) -> p n r", r=BH), ACT.Copy).then_inc(s_en, 1)
            act.wait_ge(s_oned, 1)
            act.wait_ge(s_scr, 16 * 2 * NPART)

            def values(turn, u, first=False):
                act.wait_ge(s_bl[u], turn * 80 + 80)
                if not first:
                    act.wait_ge(s_pv, 1 + turn * (2 * NH) + u * NH - NH)
                act.activation(cv[:, u, :, 0:NH, 0:DH], ctx_s[:, u].rearrange("p t (h e) -> p t h e", h=NH), ACT.Copy).then_inc(s_cv, 1)

            def decays(turn, u, more=True):
                b = turn * 2 + u
                for h in range(NH):
                    n = turn * (2 * NH) + u * NH + h
                    act.wait_ge(s_sc, n + 1)
                    act.wait_ge(s_pm, 1 + (n - 1 if u * NH + h else n))
                    act.activation(edec[:, h % 2], bank[2 + h % 2][:], ACT.Exp).then_inc(s_ed, 1)
                    if h == NH // 2 and more:
                        values(turn + u, 1 - u)
                act.wait_ge(s_pv, 1 + b * NH + NH)
                act.wait_ge(s_ra, 1 + turn * 2)
                act.activation(num[:, u, 0], bank[4][:, 0:HV].rearrange("p (h e) -> p h e", h=NH), ACT.Copy).then_inc(s_n0, 1)
                act.wait_ge(s_num, 1 + b + 1)
                act.wait_ge(s_n0, 1 + b + 1)
                act.wait_ge(s_ra, 1 + b)
                act.activation(sq[:], num[:, u, :, :, 0:DH], ACT.Square).then_inc(s_sqr, 1)

            values(0, 0, first=True)
            with act.Fori(0, B // 2 - 1) as it:
                decays(it, 0)
                decays(it, 1)
            decays(B // 2 - 1, 0)
            decays(B // 2 - 1, 1, more=False)
            act.wait_ge(s_st3, B)
            with act.Fori(0, B // 2) as it:

                def upper(u):
                    for k in range(KT):
                        act.wait_ge(s_xp, 1 + it * 4 + 2 * u + k + 1)
                        act.wait_ge(s_fo, 1 + it * (2 * FT))
                        act.activation(x3h[:, u, k], bank[k][:], ACT.Copy).then_inc(s_xh, 1)

                upper(0)
                for u in range(2):
                    for f in range(FT):
                        n = it * (2 * FT) + u * FT + f
                        if u == 0 and f == 1:
                            upper(1)
                        act.wait_ge(s_fp, n + 1)
                        act.wait_ge(s_fl, 1 + (n - 2 if u * FT + f > 1 else it * (2 * FT)))
                        act.activation(ff[:, f % 3], bank[2 + f % 4][:], ACT.Relu, bias=b1_col[:, f:f + 1]).then_inc(s_fr, 1)

        @block.tensor
        def _(pe):
            for s in (s_yu, s_hp, s_x, s_op, s_tp, s_vp, s_gt, s_gg, s_sp, s_pv, s_fo, s_xp):
                pe.sem_inc(s, 1)
            def begin(job):
                if job >= 8:
                    pe.wait_ge(s_prepc, copies(job - 8))
                return bank[job % 8]

            pe.wait_ge(s_zero, 6)
            pe.wait_ge(s_ldw, 16 * N_LDW)
            for i in range(WIN_JOBS):
                ps = begin(i)
                for k in range(KT):
                    for r in range(2):
                        last = pe.transpose(ps[:, (2 * k + r) * P:(2 * k + r + 1) * P],
                                            w_nat[:, 2 * i + r, k * P:(k + 1) * P], ident[:])
                last.then_inc(s_prep, 1)
            ps = begin(J_WOUT)
            for k in range(KT):
                for r in range(KT):
                    last = pe.transpose(ps[:, (2 * k + r) * P:(2 * k + r + 1) * P], wo_nat[:, r, k * P:(k + 1) * P], ident[:])
            last.then_inc(s_prep, 1)
            ps = begin(J_GATE)
            for k in range(6):
                last = pe.transpose(ps[:, k * 2 * NH:(k + 1) * 2 * NH], g_nat[:, k * P:(k + 1) * P],
                                    ident[0:2 * NH, 0:2 * NH])
            last.then_inc(s_prep, 1)
            ps = begin(J_F2)
            pe.wait_ge(s_ldf, 16 * N_LDF)
            for k in range(KT):
                last = pe.transpose(ps[:, k * P:(k + 1) * P], f2_nat[:, k].rearrange("p o h -> p (o h)"), ident[:])
            last.then_inc(s_prep, 1)
            pe.wait_ge(s_silu, 1)
            for i, (c0, c1) in enumerate(FS_COLS):
                ps = begin(J_FS + i)
                for t in range(NT):
                    last = pe.matmul(ps[:, 0:c1 - c0], feat[:, t], h_fwd[:, t, c0:c1], start=(t == 0), stop=(t == NT - 1))
                last.then_inc(s_prep, 1)
            pe.wait_ge(s_prepc, copies(J_FS + len(FS_COLS) - 1))
            for n in range(NS):
                ps = begin(J_H + n)
                for o in range(ORDER):
                    half = ps[:, o * D:(o + 1) * D]
                    pe.matmul(half, fs_t[:, n * P:(n + 1) * P], f2_z[:, o], start=True, stop=False)
                    last = pe.matmul(half, fsum[:, n * P:(n + 1) * P], fb2[:, o], start=False, stop=True)
                last.then_inc(s_prep, 1)
            ps = begin(J_SUM)
            pe.wait_ge(s_qabs, 2)
            pe.matmul(ps[:, 0:2], ones[:], qsum[:], start=True, stop=True).then_inc(s_prep, 1)
            for i in range(FT // 2):
                ps = begin(J_W1 + i)
                pe.wait_ge(s_quant, 1)
                for k in range(KT):
                    for r in range(2):
                        last = pe.transpose(ps[:, (2 * k + r) * P:(2 * k + r + 1) * P],
                                            w1_nat[:, 2 * i + r, k * P:(k + 1) * P], ident[:])
                last.then_inc(s_prep, 1)
            for i in range(FT // 2):
                ps = begin(J_W2 + i)
                pe.wait_ge(s_quant, 2)
                for r in range(2):
                    for k in range(KT):
                        last = pe.transpose(ps[:, (2 * r + k) * P:(2 * r + k + 1) * P],
                                            w2_nat[:, k, (2 * i + r) * P:(2 * i + r + 1) * P], ident[:])
                last.then_inc(s_prep, 1)
            pe.wait_ge(s_prepc, copies(JOBS - 1))
            pe.wait_ge(s_ldt, 32)

            with pe.Fori(0, STEPS) as it:
                tile0 = it * (ORDER * FJ)

                for q in range(4):
                    b, k = q // KT, q % KT
                    pe.wait_ge(s_res, 1 + it * 4)
                    pe.wait_ge(s_xn, it * (PB * NT) + (b + 1) * NT)
                    for t in range(NT):
                        last = pe.transpose(bank[q][:, t * P:(t + 1) * P], xn[:, b * NT + t, k * P:(k + 1) * P], ident[:])
                    last.then_inc(s_tp, 1)
                pe.wait_ge(s_xf, 1 + it * 2 + 2)
                pe.wait_ge(s_v2, 1 + it * 4)
                for q in range(4):
                    pm, nt = q // 2, q % 2
                    for b in range(PB):
                        for k in range(KT):
                            last = pe.matmul(bank[4 + q][:, b * D:(b + 1) * D], xf[:, pm, k, b, nt * P:(nt + 1) * P],
                                             win_t[:, k, 0:D], start=(k == 0), stop=(k == KT - 1))
                    last.then_inc(s_vp, 1)
                pe.wait_ge(s_xt, 1 + it * 4 + 4)
                for q in range(4):
                    back, nt = q // 2, q % 2
                    for b in range(PB):
                        for k in range(KT):
                            t0 = back * HALF + nt * P
                            last = pe.matmul(bank[q][:, b * D:(b + 1) * D],
                                             xn_t[:, k, b, t0:t0 + P],
                                             win_t[:, k, D:2 * D], start=(k == 0), stop=(k == KT - 1))
                    last.then_inc(s_gp, 1)
                for q in range(4):
                    b, dh = q // KT, q % KT
                    pe.wait_ge(s_vf, it * 4 + q + 1)
                    for k in range(KT):
                        last = pe.matmul(bank[4 + q][:], win_t[:, k, 2 * D + dh * P:2 * D + (dh + 1) * P],
                                         xn_t[:, k, b], start=(k == 0), stop=(k == KT - 1))
                    last.then_inc(s_hp, 1)

                def forward(o, j):
                    g = o * FJ + j
                    if g >= 2:
                        pe.wait_ge(s_xu, tile0 + g - 1)
                    is_even = j < FJ // 2
                    for cs in range(2):
                        pm = cs if is_even else 1 - cs
                        for nt in range(2):
                            last = pe.matmul(bank[2 * (g % 2) + cs][:], fwd[:, nt, j, cs], vf[:, pm, nt],
                                             start=(nt == 0), stop=(nt == 1))
                    last.then_inc(s_x, 1)

                def part(j, cs):
                    return cs if j < FJ // 2 else 1 - cs

                def backward1(j):
                    pe.wait_ge(s_y, 1 + tile0 + j + 1)
                    for cs in range(2):
                        for nt in range(2):
                            last = pe.matmul(bank[4 + 2 * part(j, cs) + nt][:], inv[:, j, cs, nt * P:(nt + 1) * P],
                                             spec[:, j % 2, cs], start=(j == 0), stop=(j == FJ - 1))
                    last.then_inc(s_yu, 1)

                def backward2(j):
                    pe.wait_ge(s_y, 1 + tile0 + FJ + j + 1)
                    for cs in range(2):
                        odd = part(j, cs)
                        for q in range(4):
                            last = pe.matmul(bank[4 + q][:, odd * HALF:(odd + 1) * HALF],
                                             spec[:, j % 2, cs, q * P:(q + 1) * P], inv[:, j, cs],
                                             start=(j == 0 and cs == 0), stop=(j == FJ - 1), skip_group_check=True)
                    last.then_inc(s_yu, 1)

                pe.wait_ge(s_g1, it * 4 + 4)
                forward(0, 0)
                forward(0, 1)
                pe.wait_ge(s_g2, it * 4 + 4)
                for j in range(FJ):
                    backward1(j)
                    if j + 2 < FJ:
                        forward(0, j + 2)
                pe.wait_ge(s_v1, it * 2 + 2)
                forward(1, 0)
                forward(1, 1)
                pe.wait_ge(s_ev1, it * 2 + 2)
                pe.wait_ge(s_u, it * 2 + 2)
                for j in range(FJ):
                    backward2(j)
                    if j + 2 < FJ:
                        forward(1, j + 2)
                pe.wait_ge(s_xu, tile0 + ORDER * FJ)
                for q in range(4):
                    b = q // 2
                    pe.wait_ge(s_v2, 1 + it * 4 + 2 * b + 2)
                    for r in range(2):
                        t = 2 * (q % 2) + r
                        for k in range(KT):
                            last = pe.matmul(bank[q][:, r * D:(r + 1) * D], v2_t[:, b, k, t * P:(t + 1) * P],
                                             wout_t[:, k], start=(k == 0), stop=(k == KT - 1))
                    last.then_inc(s_op, 1)
            with pe.Fori(0, B // 2) as it:
                for u in range(2):
                    pe.wait_ge(s_gv, 1 + it * 2)
                    pe.wait_ge(s_gx, 1 + it * 8)
                    pe.wait_ge(s_qn, it * 2 + u + 1)
                    for q in range(2 * KT):
                        if q == KT:
                            pe.wait_ge(s_cl[u], it * 16 + 16)
                        src = (qn if q < KT else ctx_s)[:, u]
                        k = q % KT
                        for t in range(NT):
                            last = pe.transpose(bank[4 * u + q][:, t * P:(t + 1) * P], src[:, t, k * P:(k + 1) * P], ident[:])
                        last.then_inc(s_gt, 1)
                for u in range(2):
                    pe.wait_ge(s_gx, 1 + it * 8 + 4 * u + 4)
                    for t in range(NT):
                        for q in range(2 * KT):
                            k = q % KT
                            src, w = (q_t, wg_t) if q < KT else (k_t, wkv)
                            last = pe.matmul(bank[4 * u][:, t * 2 * NH:(t + 1) * 2 * NH], src[:, u, k, t * P:(t + 1) * P], w[:, k],
                                             start=(q == 0), stop=(q == 2 * KT - 1))
                    last.then_inc(s_gg, 1)
            pe.wait_ge(s_gv, 1 + B)
            pe.wait_ge(s_gx, 1 + 4 * B)
            for i in range(2):
                for t in range(NT):
                    last = pe.transpose(bank[i][0:BH, t * P:(t + 1) * P], gates[:, t, i].rearrange("p b h -> p (b h)"), ident[:])
                last.then_inc(s_rows, 1)
            pe.wait_ge(s_ek, 1)
            for i, (n0, n1) in enumerate(((0, 8), (8, NEN))):
                for n in range(n0, n1):
                    last = pe.transpose(bank[2 + i][:, (n - n0) * BH:(n - n0 + 1) * BH], ek[:, n], ident[0:BH, 0:BH])
                last.then_inc(s_ent, 1)
            pe.wait_ge(s_en, 2)
            pe.wait_ge(s_idb, 1)
            pe.wait_ge(s_ldm, 48)
            with pe.Fori(0, B // 2) as it:
                for u in range(2):
                    b = it * 2 + u

                    def scores(h):
                        n = it * (2 * NH) + u * NH + h
                        rows = slice(DH * (h % (P // DH)), DH * (h % (P // DH)) + DH)
                        k = h // (P // DH)
                        pe.wait_ge(s_pm, 1 + (n - 1 if u * NH + h else n))
                        for c in range(NT):
                            t = slice(c * P, (c + 1) * P)
                            pe.matmul(bank[h % 2][:, t], k_t[rows, u, k, t], q_t[rows, u, k, t], start=True, stop=True)
                        pe.matmul(bank[2 + h % 2][:], identb[:], mask[:], start=True, stop=False)
                        pe.matmul(bank[2 + h % 2][:], a_st[:, u, h], m_mv[:, u, h], start=False, stop=True).then_inc(s_sc, 1)

                    pe.wait_ge(s_bl[u], it * 80 + 80)
                    scores(0)
                    scores(1)
                    pe.wait_ge(s_vs, 1 + b + 1)
                    pe.wait_ge(s_num, 1 + b)
                    pe.wait_ge(s_n0, 1 + b)
                    for k in range(KT):
                        for c in range(NT - 1):
                            for j in range(c + 1):
                                last = pe.matmul(bank[4 + k][:, c * GV:(c + 1) * GV], ctx_s[:, u, j, k * P:(k + 1) * P],
                                                 vs[:, c * (c + 1) // 2 + j].rearrange("p h e -> p (h e)")[:, k * GV:(k + 1) * GV],
                                                 start=(j == 0), stop=(j == c))
                        last.then_inc(s_sp, 1)
                    pe.wait_ge(s_bd, b * 2 + 2)
                    for c in range(1, NT):
                        for k in range(KT):
                            last = pe.matmul(bank[4 + c][:, k * GV:(k + 1) * GV], q_t[:, u, k, c * P:(c + 1) * P], bd[:, k, c - 1],
                                             start=True, stop=True)
                        last.then_inc(s_ip, 1)
                    pe.wait_ge(s_in, b * (NT - 1) + NT - 1)
                    for h in range(NH):
                        pe.wait_ge(s_pm, 1 + it * (2 * NH) + u * NH + h + 1)
                        for c in range(NT):
                            last = pe.matmul(bank[4 + c][:, h * V1:(h + 1 + PADH) * V1], pmat[:, h % 2, c * P:(c + 1) * P],
                                             cv[:, u, c, h:h + 1 + PADH].rearrange("p h e -> p (h e)"), start=True, stop=True)
                        last.then_inc(s_pv, 1)
                        if h + 2 < NH:
                            scores(h + 2)
            with pe.Fori(0, B // 2) as it:

                def turn(u):
                    pe.wait_ge(s_x3, it * 2 + u + 1)
                    pe.wait_ge(s_xl, 1 + it * 4 + 2 * u)
                    for k in range(KT):
                        for t in range(NT):
                            last = pe.transpose(bank[k][:, t * P:(t + 1) * P], x3[:, u, t, k * P:(k + 1) * P], ident[:])
                        last.then_inc(s_xp, 1)

                def hidden(u, f):
                    n = it * (2 * FT) + u * FT + f
                    pe.wait_ge(s_fr, 1 + (n - 3 if u * FT + f > 2 else it * (2 * FT)))
                    for k in range(KT):
                        for i, part_ in enumerate((x3h, x3l)):
                            last = pe.matmul(bank[2 + f % 4][:], wq1_t[:, k, f * P:(f + 1) * P], part_[:, u, k],
                                             start=(k == 0 and i == 0), stop=(k == KT - 1 and i == 1))
                    last.then_inc(s_fp, 1)

                turn(0)
                for u in range(2):
                    pe.wait_ge(s_xl, 1 + it * 4 + 2 * u + 2)
                    hidden(u, 0)
                    hidden(u, 1)
                    if u == 0:
                        turn(1)
                    pe.wait_ge(s_ob, 1 + it * 4 + 2 * u)
                    for f in range(FT):
                        if f + 2 < FT:
                            hidden(u, f + 2)
                        n = it * (2 * FT) + u * FT + f
                        for i, part_ in enumerate((ffh, ffl)):
                            if i == 0:
                                pe.wait_ge(s_fh, n + 1)
                            else:
                                pe.wait_ge(s_fl, 1 + n + 1)
                            for t in range(NT):
                                last = pe.matmul(bank[6 + t // 2][:, (t % 2) * D:(t % 2 + 1) * D], part_[:, f % 4, t * P:(t + 1) * P],
                                                 wq2_t[:, f], start=(f == 0 and i == 0 and t % 2 == 0),
                                                 stop=(f == FT - 1 and i == 1), skip_group_check=True)
                        last.then_inc(s_fo, 1)

        @block.vector
        def _(dve):
            for s in (s_xf, s_v2, s_res, s_gv, s_pm, s_ra, s_num, s_ob, s_fl, s_xl):
                dve.sem_inc(s, 1)
            own = Count(dve, own_p)
            dve.wait_ge(s_ldf, 16 * N_LDF)
            for t in range(NT):
                dve.scalar_tensor_tensor(feat[:, t], fw1_bc[:], time[:, t:t + 1], fb1_bc[:], ALU.mult, ALU.add).then_inc(s_feat, 1)
            dve.wait_ge(s_ldx, 16 * B)
            for i in range(TILES):
                last = dve.bn_stats(stats[:, i], res[:, i])
            own.then(last)
            for i in range(TILES):
                last = dve.bn_aggr(mv[:, i], stats[:, i])
            own.then(last)
            own.then(dve.tensor_scalar(var_eps[:], mv[:, :, 1], LN_EPS, None, ALU.add))
            inverse_root(own, dve, rstd[:], var_eps[:], nwt[:])
            dve.wait_ge(s_ldq, 16 * N_LDQ)
            w1_flat = w1_nat[:].rearrange("p i c -> p (i c)")
            w2_flat = w2_nat[:].rearrange("p i c -> p (i c)")
            for i, flat in enumerate((w1_flat, w2_flat)):
                dve.tensor_reduce(qsum[:, i:i + 1], flat, AX_X, ALU.add, apply_absolute_value=True).then_inc(s_qabs, 1)
            own.then(dve.tensor_scalar(gain[:], gain[:], 1.0, None, ALU.add))
            dve.wait_ge(s_prep, J_SUM + 1)
            own.then(dve.tensor_scalar(qden[:], bank[J_SUM % 8][:, 0:2], 1.0 / (FF * D), Q_EPS, ALU.mult, ALU.add))
            own.then(dve.reciprocal(qrec[:], qden[:]))
            for i, flat in enumerate((w1_flat, w2_flat)):
                own.then(dve.tensor_scalar(flat, flat, qrec[:, i:i + 1], 1.0, ALU.mult, ALU.min))
                own.then(dve.tensor_scalar(flat, flat, -1.0, ROUND, ALU.max, ALU.add))
                dve.tensor_scalar(flat, flat, -ROUND, None, ALU.add).then_inc(s_quant, 1)
            dve.wait_ge(s_prep, JOBS)
            dve.wait_ge(s_prepc, copies(JOBS - 1))

            own = Count(dve, own_a)
            OWN_A = 2
            with dve.Fori(0, STEPS) as it:
                own.from_(it * OWN_A)
                dve.wait_ge(s_tp, 1 + it * 4)
                for i in range(PB * NT):
                    one = ds(it * (PB * NT) + i, 1)
                    dve.tensor_scalar(xn[:, i:i + 1], res[:, one], mv[:, one, 0], rstd[:, one],
                                      ALU.subtract, ALU.mult).then_inc(s_xn, 1)
                dve.wait_ge(s_xt, 1 + it * 4 + 4)
                dve.wait_ge(s_vp, 1 + it * 4)
                for pm, op in enumerate((ALU.add, ALU.subtract)):
                    dve.tensor_tensor(xf[:, pm], xn_t[:, :, :, 0:HALF], xn_t[:, :, :, HALF:L], op).then_inc(s_xf, 1)

                def products(o, j):
                    g = o * FJ + j
                    tile = it * (ORDER * FJ) + g
                    dve.wait_ge(s_x, 1 + tile + 1)
                    dve.wait_ge(s_y, 1 + (tile - 1 if g else it * (ORDER * FJ)))
                    xc, xs = (bank[2 * (g % 2) + cs][:].rearrange("p (b d) -> p b d", b=PB) for cs in range(2))
                    h = [filt[:, o, n].unsqueeze(1).to_broadcast([P, PB, D]) for n in (j, FJ + j, 2 * FJ if j == 0 else j)]
                    for i, (spectrum, filter_) in enumerate(((xc, h[0]), (xs, h[1]), (xs, h[2]), (xc, h[1]))):
                        last = dve.tensor_tensor(prod[:, g % 2, i].rearrange("p (b d) -> p b d", b=PB), spectrum,
                                                 filter_, ALU.mult)
                    last.then_inc(s_xu, 1)

                for j in range(FJ):
                    products(0, j)
                dve.wait_ge(s_x, 1 + it * (ORDER * FJ) + FJ)
                for nt in range(2):
                    dve.wait_ge(s_ev1, it * 2 + nt + 1)
                    odd = bank[6 + nt][:]
                    dve.tensor_tensor(ysum[:, nt, 0], even[:, nt], odd, ALU.add)
                    dve.tensor_tensor(ysum[:, nt, 1], even[:, nt], odd, ALU.subtract).then_inc(s_u, 1)
                for nt in range(2):
                    dve.wait_ge(s_u, it * 2 + nt + 1)
                    dve.tensor_tensor(ysum[:, nt, 0], ysum[:, nt, 0], g1[:, 0, nt], ALU.mult)
                    own.then(dve.tensor_tensor(ysum[:, nt, 1], ysum[:, nt, 1], g1[:, 1, nt], ALU.mult))
                    dve.tensor_tensor(vf[:, 0, nt], ysum[:, nt, 0], ysum[:, nt, 1], ALU.add)
                    dve.tensor_tensor(vf[:, 1, nt], ysum[:, nt, 0], ysum[:, nt, 1], ALU.subtract).then_inc(s_v1, 1)
                for j in range(FJ):
                    products(1, j)
                for q in range(4):
                    dve.wait_ge(s_ev2, it * 4 + q + 1)
                    odd = bank[4 + q][:, HALF:L]
                    dve.tensor_tensor(ysum_q[:, q, 0], even_q[:, q], odd, ALU.add)
                    dve.tensor_tensor(ysum_q[:, q, 1], even_q[:, q], odd, ALU.subtract).then_inc(s_u2, 1)
                for q in range(4):
                    b, dh = q // KT, q % KT
                    dve.wait_ge(s_u2, it * 4 + q + 1)
                    dve.tensor_tensor(v2_t[:, b, dh, 0:HALF], ysum_q[:, q, 0], g2_t[:, b, dh, 0:HALF], ALU.mult)
                    dve.tensor_tensor(v2_t[:, b, dh, L - 1:HALF - 1:-1], ysum_q[:, q, 1],
                                      g2_t[:, b, dh, HALF:L], ALU.mult).then_inc(s_v2, 1)
                for q in range(4):
                    two = ds(it * (PB * NT) + 2 * q, 2)
                    dve.wait_ge(s_op, 1 + it * 4 + q + 1)
                    dve.tensor_tensor(res[:, two], res[:, two], bank[q][:].rearrange("p (t d) -> p t d", t=2),
                                      ALU.add).then_inc(s_res, 1)
                for q in range(4):
                    dve.wait_ge(s_res, 1 + it * 4 + q + 1)
                    for r in range(2):
                        one = ds(it * (PB * NT) + 2 * q + r, 1)
                        last = dve.bn_stats(stats[:, one], res[:, one])
                last.then_inc(s_st2, 1)
                assert own.n == OWN_A
            def token_roots():
                for i in range(TILES):
                    last = dve.bn_aggr(mv[:, i], stats[:, i])
                own.then(last)
                own.then(dve.tensor_scalar(var_eps[:], mv[:, :, 1], LN_EPS, None, ALU.add))
                inverse_root(own, dve, rstd[:], var_eps[:], nwt[:])

            own = Count(dve, own_n)
            dve.wait_ge(s_st2, STEPS)
            token_roots()
            own.then(dve.tensor_tensor(wkv[:], wg_t[:, KT:2 * KT], wg_t[:, 2 * KT:3 * KT], ALU.add))
            with dve.Fori(0, B // 2) as it:
                for u in range(2):
                    dve.wait_ge(s_gt, 1 + it * 8)
                    for t in range(NT):
                        one = ds(it * (2 * NT) + u * NT + t, 1)
                        last = dve.tensor_scalar(qn[:, u, t:t + 1], res[:, one], mv[:, one, 0], rstd[:, one], ALU.subtract, ALU.mult)
                    last.then_inc(s_qn, 1)
                for u in range(2):
                    dve.wait_ge(s_gg, 1 + it * 2 + u + 1)
                    dve.tensor_copy(gates[:, :, :, ds(it * 2 + u, 1)],
                                    bank[4 * u][:, 0:NT * 2 * NH].rearrange("p (t i b h) -> p t i b h", t=NT, i=2, b=1)).then_inc(s_gv, 1)

            own = Count(dve, own_s)
            dve.wait_ge(s_bgl, 16 * 2 * B)
            dve.tensor_scalar(bg[:], bg[:], 1.0 / CAP, None, ALU.mult).then_inc(s_bg, 1)
            dve.wait_ge(s_tanh, 2)
            own.then(dve.tensor_scalar(th[:], th[:], CAP, None, ALU.mult))
            dve.scalar_tensor_tensor(sg[:, 0], th[:, 1], -1.0, th[:, 1], ALU.mult, ALU.max).then_inc(s_absf, 1)
            dve.wait_ge(s_expf, 1)
            dve.tensor_scalar(sg[:, 2], sg[:, 1], 1.0, None, ALU.add).then_inc(s_onep, 1)
            dve.wait_ge(s_onep, 1)
            own.then(dve.tensor_scalar(sg[:, 4], sg[:, 2], -1.0, None, ALU.add))
            own.then(dve.tensor_scalar(sg[:, 5], sg[:, 4], 1e-10, None, ALU.max))
            own.then(dve.reciprocal(sg[:, 5], sg[:, 5]))
            own.then(dve.tensor_scalar(sg[:, 4], sg[:, 4], 0.0, None, ALU.is_equal))
            dve.wait_ge(s_lnp, 1)
            own.then(dve.tensor_tensor(sg[:, 3], sg[:, 3], sg[:, 5], ALU.mult))
            own.then(dve.tensor_tensor(sg[:, 3], sg[:, 3], sg[:, 4], ALU.add))
            own.then(dve.tensor_tensor(sg[:, 3], sg[:, 3], sg[:, 1], ALU.mult))
            own.then(dve.scalar_tensor_tensor(sg[:, 0], th[:, 1], 0.0, sg[:, 3], ALU.min, ALU.subtract))
            dve.wait_ge(s_one, 1)
            own.then(dve.tensor_tensor_scan(lf[:], onesrow[:], sg[:, 0], 0.0, ALU.mult, ALU.add))
            own.then(dve.tensor_tensor(aw[:], th[:, 0], lf[:], ALU.subtract))
            own.then(dve.tensor_tensor_scan(mx[:], aw[:], aw[:], -3e38, ALU.max, ALU.max))
            dve.tensor_scalar(nmx[:], mx[:], -1.0, None, ALU.mult).then_inc(s_mx, 1)
            dve.tensor_tensor(msum[:], lf[:], mx[:], ALU.add).then_inc(s_ms, 1)
            dve.wait_ge(s_mx, 1)
            for parts, whole, r in ((ap3, aw, 0), (mp3, nmx, 2)):
                own.then(dve.tensor_copy(parts[:, 0], whole[:]))
                own.then(dve.tensor_tensor(rem[:, r], whole[:], parts[:, 0], ALU.subtract))
                own.then(dve.tensor_copy(parts[:, 1], rem[:, r]))
                own.then(dve.tensor_tensor(rem[:, r + 1], rem[:, r], parts[:, 1], ALU.subtract))
                dve.tensor_copy(parts[:, 2], rem[:, r + 1]).then_inc(s_parts, 1)

            own = Count(dve, own_b)
            OWN_B = 21
            FINISH = 7
            dve.wait_ge(s_en, 2)
            dve.wait_ge(s_scr, 16 * 2 * NPART)
            dve.wait_ge(s_lda, 16)

            def finish(b, u, step):
                row = ds(b * NH, NH)
                total = num[:, u, :, :, DH]
                den, rden, ms, v, tmp, f = (tiny[:, i] for i in range(6))
                flat = hout[:].rearrange("p t h e -> p t (h e)")
                if step == 0:
                    own.from_(b * OWN_B)
                    own.then(dve.scalar_tensor_tensor(den, total, -1.0, total, ALU.mult, ALU.max))
                    own.then(dve.tensor_tensor(den, den, en[:, PAIRS + NT - 1:NEN, row], ALU.max))
                    own.then(dve.tensor_scalar(den, den, DEN_EPS, None, ALU.add))
                    own.then(dve.reciprocal(rden, den))
                elif step == 1:
                    dve.wait_ge(s_sqr, b + 1)
                    own.then(dve.tensor_reduce(ms, sq[:], AX_X, ALU.add))
                elif step == 2:
                    own.then(dve.tensor_tensor(ms, ms, rden, ALU.mult))
                    own.then(dve.tensor_tensor(ms, ms, rden, ALU.mult))
                    own.then(dve.tensor_scalar(v, ms, 1.0 / DH, RMS_EPS, ALU.mult, ALU.add))
                    inverse_root(own, dve, f, v, tmp)
                    own.then(dve.tensor_tensor(f, f, rden, ALU.mult))
                elif step == 3:
                    own.then(dve.tensor_tensor(hout[:], num[:, u, :, :, 0:DH], f.unsqueeze(3).to_broadcast([P, NT, NH, DH]), ALU.mult))
                elif step == 4:
                    own.then(dve.tensor_tensor(flat, flat, gain[:].unsqueeze(1).to_broadcast([P, NT, D]), ALU.mult))
                    assert own.n == OWN_B
                elif step == 5:
                    dve.tensor_tensor(res[:, ds(b * NT, NT)], res[:, ds(b * NT, NT)], flat, ALU.add).then_inc(s_ra, 1)
                else:
                    dve.wait_ge(s_ra, 1 + b + 1)
                    for t in range(NT):
                        last = dve.bn_stats(stats[:, ds(b * NT + t, 1)], res[:, ds(b * NT + t, 1)])
                    last.then_inc(s_st3, 1)

            def batch(turn, u, before=None):
                b = turn * 2 + u
                row = ds(b * NH, NH)
                for k in range(KT):
                    dve.wait_ge(s_sp, 1 + b * 2 + k + 1)
                    dve.tensor_tensor(bd[:, k], bank[4 + k][:, 0:(NT - 1) * GV].rearrange("p (c e) -> p c e", c=NT - 1),
                                      heads[:].unsqueeze(1).to_broadcast([P, NT - 1, GV]), ALU.mult).then_inc(s_bd, 1)
                for c in range(1, NT):
                    dve.wait_ge(s_ip, b * (NT - 1) + c)
                    w = en[:, PAIRS + c - 1, row].unsqueeze(2).to_broadcast([P, NH, V1])
                    dve.tensor_tensor(inter[:, c - 1], bank[4 + c][:, 0:HV].rearrange("p (h e) -> p h e", h=NH), w,
                                      ALU.mult).then_inc(s_in, 1)
                for h in range(NH):
                    n = turn * (2 * NH) + u * NH + h
                    dve.wait_ge(s_ed, n + 1)
                    dve.wait_ge(s_pv, 1 + (n - 1 if u * NH + h else n))
                    dve.scalar_tensor_tensor(pmat[:, h % 2], bank[h % 2][:], float(DH) ** -0.5, edec[:, h % 2], ALU.mult,
                                             ALU.mult).then_inc(s_pm, 1)
                    if before is not None and h < FINISH:
                        finish(before, 1 - u, h)
                dve.wait_ge(s_pv, 1 + b * NH + NH)
                dve.wait_ge(s_in, b * (NT - 1) + NT - 1)
                for c in range(1, NT):
                    last = dve.tensor_tensor(num[:, u, c], bank[4 + c][:, 0:HV].rearrange("p (h e) -> p h e", h=NH),
                                             inter[:, c - 1], ALU.add)
                last.then_inc(s_num, 1)
                dve.wait_ge(s_num, 1 + b + 1)
                dve.wait_ge(s_n0, 1 + b + 1)

            batch(0, 0)
            with dve.Fori(0, B // 2 - 1) as it:
                batch(it, 1, it * 2)
                batch(it + 1, 0, it * 2 + 1)
            batch(B // 2 - 1, 1, B - 2)
            for step in range(FINISH):
                finish(B - 1, 1, step)
            own = Count(dve, own_f)
            dve.wait_ge(s_st3, B)
            token_roots()
            with dve.Fori(0, B // 2) as it:

                def normalise(u):
                    dve.wait_ge(s_xp, 1 + it * 4)
                    for t in range(NT):
                        one = ds(it * (2 * NT) + u * NT + t, 1)
                        last = dve.tensor_scalar(x3[:, u, t:t + 1], res[:, one], mv[:, one, 0], rstd[:, one], ALU.subtract, ALU.mult)
                    last.then_inc(s_x3, 1)

                def lower(u):
                    for k in range(KT):
                        dve.wait_ge(s_xh, it * 4 + 2 * u + k + 1)
                        dve.wait_ge(s_fo, 1 + it * (2 * FT))
                        dve.tensor_tensor(x3l[:, u, k], bank[k][:], x3h[:, u, k].bitcast(F32), ALU.subtract).then_inc(s_xl, 1)

                normalise(0)
                normalise(1)
                lower(0)
                for u in range(2):
                    for f in range(FT):
                        n = it * (2 * FT) + u * FT + f
                        if u == 0 and f == 1:
                            lower(1)
                        dve.wait_ge(s_fr, 1 + n + 1)
                        dve.wait_ge(s_fo, 1 + (n - 3 if u * FT + f > 2 else it * (2 * FT)))
                        dve.tensor_copy(ffh[:, f % 4], ff[:, f % 3]).then_inc(s_fh, 1)
                        dve.wait_ge(s_fh, n + 1)
                        dve.tensor_tensor(ffl[:, f % 4], ff[:, f % 3], ffh[:, f % 4].bitcast(F32), ALU.subtract).then_inc(s_fl, 1)
                    dve.wait_ge(s_fo, 1 + it * (2 * FT) + (u + 1) * FT)
                    dve.wait_ge(s_rb, it * 2 + u + 1)
                    dve.wait_ge(s_so[u], 1 + it * 16)
                    for i in range(2):
                        dve.tensor_tensor(ob[:, u, 2 * i:2 * i + 2], rb[:, u, 2 * i:2 * i + 2],
                                          bank[6 + i][:].rearrange("p (t d) -> p t d", t=2), ALU.add).then_inc(s_ob, 1)


_INS = ['x', 'ctx_1024', 'L0_attn_W_in', 'L0_attn_W_out', 'L0_attn_f_w1', 'L0_attn_f_b1', 'L0_attn_f_w2',
        'L0_attn_f_b2', 'L0_xattn_ifgate_w', 'L0_xattn_ifgate_b', 'L0_xattn_outnorm_w', 'L0_ffn_W1', 'L0_ffn_b1',
        'L0_ffn_W2', 'L0_ffn_b2']


def kernel(**inputs):
    import concourse.bacc as bacc
    from concourse.bass_utils import run_bass_kernel_spmd

    nc = bacc.Bacc("TRN2", target_bir_lowering=False, num_devices=1)
    arrays = {f"in_{name}_dram": np.ascontiguousarray(inputs[name]) for name in _INS}
    for name, table in tables().items():
        arrays[f"table_{name}_dram"] = table
    args = [nc.dram_tensor(name, a.shape, mybir.dt.from_np(a.dtype), kind="ExternalInput").ap()
            for name, a in arrays.items()]
    args.append(nc.dram_tensor("out_0_dram", (B, L, D), F32, kind="ExternalOutput").ap())
    decoder_layer(nc, *args)
    r = run_bass_kernel_spmd(nc, [arrays], core_ids=[0])
    return r.results[0]["out_0_dram"]
```

```python
from contextlib import ExitStack

import numpy as np

from concourse.bass import ds
from concourse import mybir

F32 = mybir.dt.float32
F32R = mybir.dt.float32r
I32 = mybir.dt.int32
BF16 = mybir.dt.bfloat16
ALU = mybir.AluOpType
ACT = mybir.ActivationFunctionType
AX_X = mybir.AxisListType.X

P = 128
B, L, D = 8, 512, 256
NT = L // P
KT = D // P
TILES = B * NT
PB = 2
STEPS = B // PB
NC = PB * D
HALF = L // 2
ORDER, HID = 2, 64
NFFT = 2 * L
FJ = 4
LN_EPS = 1e-5

NH, DH = 8, 32
BH = B * NH
CAP = 15.0
DEN_EPS, RMS_EPS = 5e-5, 1e-6
V1 = DH + 1
PADH = 2
HT = P // DH
N_BL = 5 + HT
N_SCR = 4
NPART = 3
NEG = -1e30

FF = 1024
FT = FF // P
Q_EPS = 1e-5
ROUND = 1.5 * 2.0**23


def transform_tables():
    slot = np.arange(FJ * P)
    even = slot < HALF
    k = np.where(even, 2 * slot, 2 * (slot - HALF) + 1).astype(np.float64)
    k_sin = k.copy()
    k_sin[0] = NFFT // 2
    n = np.arange(HALF) + 0.5
    cos = np.cos(2 * np.pi / NFFT * np.outer(n, k))
    sin = np.sin(2 * np.pi / NFFT * np.outer(n, k_sin))
    both = np.stack([cos.reshape(HALF, FJ, P), sin.reshape(HALF, FJ, P)], axis=2)
    fwd = both.reshape(HALF // P, P, FJ, 2, P).transpose(1, 0, 2, 3, 4)
    w = np.full(FJ * P, 2.0 / NFFT)
    w[0] = 1.0 / NFFT
    inv = (both * w.reshape(1, FJ, 1, P)).transpose(3, 1, 2, 0)
    m = np.arange(L)
    hc = np.cos(2 * np.pi / NFFT * np.outer(m, k))
    hs = np.sin(2 * np.pi / NFFT * np.outer(m, k))
    hs[:, 0] = 0.0
    hc_sin = np.cos(2 * np.pi / NFFT * np.outer(m, k_sin[:P]))
    filt = np.concatenate([hc, hs, hc_sin], axis=1)
    filt_t = filt.reshape(NT, P, -1).transpose(1, 0, 2)
    f = lambda a: np.ascontiguousarray(a, dtype=np.float32)
    return f(fwd), f(inv), f(filt_t), f(filt.sum(0)[None, :])


def attention_tables():
    s, t = np.arange(P)[:, None], np.arange(P)[None, :]
    mask = np.tile(np.where(s <= t, 0.0, NEG), (1, NT)).astype(np.float32)
    chunk = np.zeros((NPART, NT, NH, NT, P), np.float32)
    for c in range(NT):
        chunk[:, c, :, c, :] = 1.0
    return mask, chunk.reshape(NPART * NT, NH * NT * P)


def tables():
    fwd, inv, filt, fsum = transform_tables()
    mask, chunk = attention_tables()
    time = np.ascontiguousarray(np.linspace(0.0, 1.0, L, dtype=np.float32).reshape(NT, P).T)
    head = np.arange(P)[:, None] // DH == np.arange(NH // KT * V1)[None, :] // V1
    heads = (head / np.sqrt(DH)).astype(np.float32)
    return {"fwd": fwd, "inv": inv, "filt": filt, "fsum": fsum, "time": time, "mask": mask, "chunk": chunk,
            "heads": heads}


class Count:

    def __init__(self, eng, sem):
        self.eng, self.sem, self.base, self.n = eng, sem, 0, 0

    def from_(self, base):
        self.base, self.n = base, 0

    def then(self, ins):
        self.n += 1
        ins.then_inc(self.sem, 1)
        self.eng.wait_ge(self.sem, self.base + self.n)


def root_guess(own, dve, y, v):
    own.then(dve.tensor_scalar(y.bitcast(I32), v.bitcast(I32), -0.5, float(0x5F3759DF), ALU.mult, ALU.add))


def root_step(own, dve, y, v, t):
    own.then(dve.tensor_tensor(t, y, y, ALU.mult))
    own.then(dve.scalar_tensor_tensor(t, t, -0.5, v, ALU.mult, ALU.mult))
    own.then(dve.scalar_tensor_tensor(y, t, 1.5, y, ALU.add, ALU.mult))


def inverse_root(own, dve, y, v, t):
    root_guess(own, dve, y, v)
    for _ in range(3):
        root_step(own, dve, y, v, t)


def decoder_layer(nc, x, ctx, w_in, w_out, f_w1, f_b1, f_w2, f_b2, ifw, ifb, onw, w1, b1, w2, b2,
                  c_fwd, c_inv, c_filt, c_fsum, c_time, c_mask, c_chunk, c_heads, out):
    NS = 2 * FJ + 1
    FC = NS * P
    HV = NH * V1
    GV = HV // KT
    PAIRS = (NT - 1) * NT // 2
    NEN = PAIRS + (NT - 1) + NT

    main = ExitStack()
    with main:
        def put(stack, name, shape, dt=F32):
            return stack.enter_context(nc.sbuf_tensor(name, shape, dt))

        def sem(name):
            return main.enter_context(nc.semaphore(name))

        def sb(name, shape, dt=F32):
            return put(main, name, shape, dt)

        bank = [main.enter_context(nc.psum_tensor(f"bank{i}", [P, 512], F32)) for i in range(8)]
        scr_q = nc.dram_tensor("scr_q", [B, P, KT * L], F32, kind="Internal").ap()
        scr_k = nc.dram_tensor("scr_k", [B, P, KT * L], F32, kind="Internal").ap()
        scr_g = nc.dram_tensor("scr_g", [2, B, NH, L], F32, kind="Internal").ap()
        scr_a = nc.dram_tensor("scr_a", [NPART, NT, BH, P], BF16, kind="Internal").ap()
        scr_m = nc.dram_tensor("scr_m", [NPART, BH, L], BF16, kind="Internal").ap()

        res = sb("res", [P, TILES, D])
        ident = sb("ident", [P, P])
        mv = sb("mv", [P, TILES, 2])
        stats = sb("stats", [P, TILES, 6])
        rstd = sb("rstd", [P, TILES])
        var_eps = sb("var_eps", [P, TILES])
        nwt = sb("nwt", [P, TILES])
        win_t = sb("win_t", [P, KT, 3 * D])
        wout_t = sb("wout_t", [P, KT, D])
        wg_t = sb("wg_t", [P, 6, 2 * NH])
        wq1_t = sb("wq1_t", [P, KT, FF], F32R)
        wq2_t = sb("wq2_t", [P, FT, D], F32R)
        b1_col = sb("b1_col", [P, FT])
        b2_bc = sb("b2_bc", [P, D])
        gain = sb("gain", [P, D])

        pa = ExitStack()
        fwd = put(pa, "fwd", [P, 2, FJ, 2, P])
        inv = put(pa, "inv", [P, FJ, 2, HALF])
        filt = put(pa, "filt", [P, ORDER, NS, D])
        pw = ExitStack()
        w_nat = put(pw, "w_nat", [P, 6, D])
        wo_nat = put(pw, "wo_nat", [P, KT, D])
        g_nat = put(pw, "g_nat", [2 * NH, 3 * D])
        f2_nat = put(pw, "f2_nat", [P, KT, ORDER, HID])
        f2_z = put(pw, "f2_z", [P, ORDER, D])
        fw1_bc = put(pw, "fw1_bc", [P, ORDER * HID])
        fb1_bc = put(pw, "fb1_bc", [P, ORDER * HID])
        fb2 = put(pw, "fb2", [P, ORDER, D])
        feat = put(pw, "feat", [P, NT, P])
        fs_t = put(pw, "fs_t", [P, FC])
        h_fwd = put(pw, "h_fwd", [P, NT, FC])
        fsum = put(pw, "fsum", [P, FC])
        time = put(pw, "time", [P, NT])
        w1_nat = put(pw, "w1_nat", [P, FT, D])
        w2_nat = put(pw, "w2_nat", [P, KT, FF])
        qsum = put(pw, "qsum", [P, 2])
        qden = put(pw, "qden", [P, 2])
        qrec = put(pw, "qrec", [P, 2])
        ones = put(pw, "ones", [P, P])
        pw.close()
        xn = put(pa, "xn", [P, PB * NT, D])
        xn_t = put(pa, "xn_t", [P, KT, PB, L])
        xf = put(pa, "xf", [P, 2, KT, PB, HALF])
        vf = put(pa, "vf", [P, 2, 2, NC])
        g1 = put(pa, "g1", [P, 2, 2, NC])
        v2_t = g1[:].rearrange("p a b (c d) -> p (a b c d)", c=PB).rearrange("p (b k t) -> p b k t", b=PB, k=KT)
        g2_t = put(pa, "g2_t", [P, PB, KT, L])
        prod = put(pa, "prod", [P, 2, 4, NC])
        spec = put(pa, "spec", [P, 2, 2, NC])
        even = put(pa, "even", [P, 2, NC])
        even_q = even[:].rearrange("p a (b n) -> p (a b) n", b=PB)
        ysum = put(pa, "ysum", [P, 2, 2, NC])
        ysum_q = ysum[:].rearrange("p a b (c n) -> p (a b c) n", c=PB).rearrange("p (q s) n -> p q s n", s=2)
        pa.close()

        pb = ExitStack()
        ctx_s = put(pb, "ctx_s", [P, 2, NT, D])
        q_t = put(pb, "q_t", [P, 2, KT, L])
        k_t = put(pb, "k_t", [P, 2, KT, L])
        mask = put(pb, "mask", [P, L], BF16)
        identb = put(pb, "identb", [P, P], BF16)
        heads = put(pb, "heads", [P, GV])
        en = put(pb, "en", [P, NEN, BH])
        a_st = put(pb, "a_st", [NPART * NT + NPART, 2, NH, P], BF16)
        m_mv = put(pb, "m_mv", [NPART * NT + NPART, 2, NH, L], BF16)
        q_z = put(pb, "q_z", [P, 2, HT, KT, L])
        pg = ExitStack()
        qn = put(pg, "qn", [P, 2, NT, D])
        wkv = put(pg, "wkv", [P, KT, 2 * NH])
        bg = put(pg, "bg", [BH, 2])
        th = put(pg, "th", [BH, 2, L])
        sg = put(pg, "sg", [BH, 6, L])
        lf = put(pg, "lf", [BH, L])
        aw = put(pg, "aw", [BH, L])
        mx = put(pg, "mx", [BH, L])
        nmx = put(pg, "nmx", [BH, L])
        msum = put(pg, "msum", [BH, L])
        ek = put(pg, "ek", [BH, NEN, P])
        ap3 = put(pg, "ap3", [BH, NPART, L], BF16)
        mp3 = put(pg, "mp3", [BH, NPART, L], BF16)
        rem = sg
        rows = put(pg, "rows", [2 * NH, 2, L])
        onesrow = put(pg, "onesrow", [BH, L])
        pg.close()
        cv = put(pb, "cv", [P, 2, NT, NH + PADH, V1])
        edec = put(pb, "edec", [P, 2, L])
        pmat = put(pb, "pmat", [P, 2, L])
        vs = put(pb, "vs", [P, PAIRS, NH, V1])
        bd = put(pb, "bd", [P, KT, NT - 1, GV])
        inter = put(pb, "inter", [P, NT - 1, NH, V1])
        num = put(pb, "num", [P, 2, NT, NH, V1])
        sq = put(pb, "sq", [P, NT, NH, DH])
        hout = put(pb, "hout", [P, NT, NH, DH])
        tiny = put(pb, "tiny", [P, 8, NT, NH])
        pb.close()

        pc = ExitStack()
        x3 = put(pc, "x3", [P, 2, NT, D])
        x3h = put(pc, "x3h", [P, 2, KT, L], F32R)
        x3l = put(pc, "x3l", [P, 2, KT, L], F32R)
        put(pc, "kept", [P, (L + P) // 2 + GV + NEN * BH])
        ff = put(pc, "ff", [P, 3, L])
        ffh = put(pc, "ffh", [P, 4, L], F32R)
        ffl = put(pc, "ffl", [P, 4, L], F32R)
        rb = put(pc, "rb", [P, 2, NT, D])
        ob = put(pc, "ob", [P, 2, NT, D])
        pc.close()

        s_ldf = sem("s_ldf")
        s_ldx = sem("s_ldx")
        s_ldt = sem("s_ldt")
        s_ldw = sem("s_ldw")
        s_ldq = sem("s_ldq")
        s_zero = sem("s_zero")
        s_feat = sem("s_feat")
        s_silu = sem("s_silu")
        s_prep = sem("s_prep")
        s_prepc = sem("s_prepc")
        s_qabs = sem("s_qabs")
        s_quant = sem("s_quant")
        own_p = sem("own_p")
        s_xn = sem("s_xn")
        s_tp = sem("s_tp")
        s_xt = sem("s_xt")
        s_xf = sem("s_xf")
        s_vp = sem("s_vp")
        s_vf = sem("s_vf")
        s_gp = sem("s_gp")
        s_g1 = sem("s_g1")
        s_hp = sem("s_hp")
        s_g2 = sem("s_g2")
        s_x = sem("s_x")
        s_xu = sem("s_xu")
        s_y = sem("s_y")
        s_yu = sem("s_yu")
        s_ev1 = sem("s_ev1")
        s_u = sem("s_u")
        own_a = sem("own_a")
        s_v1 = sem("s_v1")
        s_ev2 = sem("s_ev2")
        s_u2 = sem("s_u2")
        s_v2 = sem("s_v2")
        s_op = sem("s_op")
        s_res = sem("s_res")
        s_st2 = sem("s_st2")
        own_n = sem("own_n")
        s_cl = [sem(f"s_cl{u}") for u in range(2)]
        s_wkv = sem("s_wkv")
        s_qn = sem("s_qn")
        s_gt = sem("s_gt")
        s_gx = sem("s_gx")
        s_gg = sem("s_gg")
        s_gv = sem("s_gv")
        s_sq = [sem(f"s_sq{u}") for u in range(2)]
        s_bgl = sem("s_bgl")
        s_bg = sem("s_bg")
        s_one = sem("s_one")
        s_sg = [sem(f"s_sg{u}") for u in range(2)]
        s_rows = sem("s_rows")
        s_tanh = sem("s_tanh")
        s_absf = sem("s_absf")
        s_expf = sem("s_expf")
        s_onep = sem("s_onep")
        s_lnp = sem("s_lnp")
        s_mx = sem("s_mx")
        s_ms = sem("s_ms")
        s_ek = sem("s_ek")
        s_ent = sem("s_ent")
        s_en = sem("s_en")
        s_parts = sem("s_parts")
        s_scr = sem("s_scr")
        s_lda = sem("s_lda")
        s_ldm = sem("s_ldm")
        s_idb = sem("s_idb")
        own_s = sem("own_s")
        s_bl = [sem(f"s_bl{u}") for u in range(2)]
        s_cv = sem("s_cv")
        s_vs = sem("s_vs")
        s_sp = sem("s_sp")
        s_bd = sem("s_bd")
        s_ip = sem("s_ip")
        s_in = sem("s_in")
        s_sc = sem("s_sc")
        s_ed = sem("s_ed")
        s_pm = sem("s_pm")
        s_pv = sem("s_pv")
        s_n0 = sem("s_n0")
        s_num = sem("s_num")
        s_sqr = sem("s_sqr")
        s_ra = sem("s_ra")
        s_st3 = sem("s_st3")
        own_b = sem("own_b")
        s_oned = sem("s_oned")
        own_f = sem("own_f")
        own_c = sem("own_c")
        s_x3 = sem("s_x3")
        s_xp = sem("s_xp")
        s_xh = sem("s_xh")
        s_xl = sem("s_xl")
        s_fp = sem("s_fp")
        s_fr = sem("s_fr")
        s_fh = sem("s_fh")
        s_fl = sem("s_fl")
        s_fo = sem("s_fo")
        s_rb = sem("s_rb")
        s_ob = sem("s_ob")
        s_so = [sem(f"s_so{u}") for u in range(2)]
        N_LDF, N_LDW, N_LDQ = 8, 3, 5
        WIN_JOBS, FS_COLS = 3, [(0, 512), (512, 1024), (1024, FC)]
        J_WOUT = WIN_JOBS
        J_GATE = J_WOUT + 1
        J_F2 = J_GATE + 1
        J_FS = J_F2 + 1
        J_H = J_FS + len(FS_COLS)
        J_SUM = J_H + NS
        J_W1 = J_SUM + 1
        J_W2 = J_W1 + FT // 2
        JOBS = J_W2 + FT // 2

        def copies(job):
            return job + 1 - (job >= J_SUM)

        block = main.enter_context(nc.Block())

        @block.sync
        def _(sp):
            for s in (*s_so, *s_sq, *s_sg):
                sp.sem_inc(s, 1)
            sp.dma_start(fw1_bc[:], f_w1.rearrange("o h a -> (o h a)").partition_broadcast(P)).then_inc(s_ldf, 16)
            sp.dma_start(fb1_bc[:], f_b1.rearrange("o h -> (o h)").partition_broadcast(P)).then_inc(s_ldf, 16)
            sp.dma_start(time[:], c_time).then_inc(s_ldf, 16)
            sp.dma_start(w_nat[:], w_in.rearrange("(i p) c -> p i c", p=P)).then_inc(s_ldw, 16)
            sp.dma_start(wo_nat[:], w_out.rearrange("(i p) c -> p i c", p=P)).then_inc(s_ldw, 16)
            sp.dma_start(g_nat[:], ifw).then_inc(s_ldw, 16)
            for o in range(ORDER):
                sp.dma_start(f2_nat[:, :, o], f_w2[o].rearrange("(k p) h -> p k h", p=P)).then_inc(s_ldf, 16)
            sp.wait_ge(s_zero, 6)
            sp.dma_start(fb2[0:1], f_b2.rearrange("(a o) d -> a o d", a=1)).then_inc(s_ldf, 16)
            sp.dma_start(fsum[0:1, :], c_fsum).then_inc(s_ldf, 16)
            sp.dma_start(h_fwd[:], c_filt).then_inc(s_ldf, 16)
            for b in range(B):
                sp.dma_start(res[:, b * NT:(b + 1) * NT, :], x[b].rearrange("(t p) d -> p t d", p=P)).then_inc(s_ldx, 16)
            sp.dma_start(fwd[:], c_fwd).then_inc(s_ldt, 16)
            sp.dma_start(inv[:], c_inv).then_inc(s_ldt, 16)
            sp.dma_start(w1_nat[:], w1.rearrange("(i p) c -> p i c", p=P)).then_inc(s_ldq, 16)
            sp.dma_start(w2_nat[:], w2.rearrange("(i p) c -> p i c", p=P)).then_inc(s_ldq, 16)
            sp.dma_start(b1_col[:], b1.rearrange("(i p) -> p i", p=P), allow_slow_non_contiguous=True).then_inc(s_ldq, 16)
            sp.dma_start(b2_bc[:], b2.partition_broadcast(P)).then_inc(s_ldq, 16)
            sp.dma_start(gain[:], onw.partition_broadcast(P)).then_inc(s_ldq, 16)
            sp.wait_ge(s_st2, STEPS)
            def load_ctx(b, u, signal):
                sp.dma_start(ctx_s[:, u], ctx[ds(b, 1)].rearrange("a (t p) d -> p (a t) d", p=P)).then_inc(signal, 16)

            def store_qk(b, u):
                sp.dma_start(scr_q[ds(b, 1)].rearrange("a p (k t) -> p (a k) t", k=KT), q_t[:, u]).then_inc(s_sq[u], 16)
                sp.dma_start(scr_k[ds(b, 1)].rearrange("a p (k t) -> p (a k) t", k=KT), k_t[:, u]).then_inc(s_sq[u], 16)

            def store_gates(b, u):
                sp.wait_ge(s_gv, 1 + b + 1)
                for i in range(2):
                    sp.dma_start(scr_g[i, ds(b, 1)].rearrange("a h t -> h (a t)"), rows[i * NH:(i + 1) * NH, u]).then_inc(s_sg[u], 16)

            for u in range(2):
                load_ctx(u, u, s_cl[u])
            for b in range(B):
                for i in range(2):
                    sp.dma_start(bg[b * NH:(b + 1) * NH, i:i + 1], ifb.rearrange("(i h a) -> i h a", i=2, a=1)[i]).then_inc(s_bgl, 16)
            sp.dma_start(heads[:], c_heads).then_inc(s_lda, 16)
            with sp.Fori(0, B // 2 - 1) as it:
                for u in range(2):
                    sp.wait_ge(s_gt, 1 + it * 8 + 4 * u + 4)
                    load_ctx(it * 2 + 2 + u, u, s_cl[u])
                    sp.wait_ge(s_gx, 1 + it * 8 + 4 * u + 4)
                    store_qk(it * 2 + u, u)
                for u in range(2):
                    store_gates(it * 2 + u, u)
            for u in range(2):
                sp.wait_ge(s_gx, 1 + 4 * (B - 2 + u) + 4)
                store_qk(B - 2 + u, u)
            for u in range(2):
                store_gates(B - 2 + u, u)
            for u in range(2):
                sp.wait_ge(s_sg[u], 1 + 32 * (B // 2))
            sp.dma_start(th[:], scr_g.rearrange("i b h t -> (b h) i t")).then_inc(s_rows, 16)

            def load_operands(b, u):
                load_ctx(b, u, s_bl[u])
                sp.dma_start(q_t[:, u], scr_q[ds(b, 1)].rearrange("a p (k t) -> p (a k) t", k=KT)).then_inc(s_bl[u], 16)
                sp.dma_start(k_t[:, u], scr_k[ds(b, 1)].rearrange("a p (k t) -> p (a k) t", k=KT)).then_inc(s_bl[u], 16)
                for j in range(HT):
                    part = slice(j * DH, (j + 1) * DH)
                    sp.dma_start(q_z[part, u, j], scr_q[ds(b, 1), part].rearrange("a p (k t) -> p (a k) t", k=KT)).then_inc(s_bl[u], 16)

            def load_exponents(b, u):
                sp.dma_start(a_st[0:NPART * NT, u], scr_a.rearrange("i c h s -> (i c) h s")[:, ds(b * NH, NH)]).then_inc(s_bl[u], 16)
                sp.dma_start(m_mv[NPART * NT:NPART * NT + NPART, u], scr_m[:, ds(b * NH, NH)]).then_inc(s_bl[u], 16)

            sp.wait_ge(s_gg, 1 + B)
            sp.wait_ge(s_one, 3)
            for u in range(2):
                sp.wait_ge(s_sq[u], 1 + 32 * (B // 2))
                load_operands(u, u)
            sp.wait_ge(s_parts, 1)
            for i in range(NPART):
                sp.dma_start(scr_a[i].rearrange("c h s -> h c s"), ap3[:, i].rearrange("h (c s) -> h c s", c=NT)).then_inc(s_scr, 16)
            sp.wait_ge(s_parts, 2)
            sp.dma_start(scr_m.rearrange("i h t -> h i t"), mp3[:]).then_inc(s_scr, 16)
            sp.wait_ge(s_scr, 16 * N_SCR)
            for u in range(2):
                load_exponents(u, u)
            with sp.Fori(0, B // 2 - 1) as it:
                for u in range(2):
                    sp.wait_ge(s_pv, 1 + it * (2 * NH) + (u + 1) * NH)
                    load_operands(it * 2 + 2 + u, u)
                    load_exponents(it * 2 + 2 + u, u)
            with sp.Fori(0, B // 2) as it:
                for u in range(2):
                    sp.wait_ge(s_ob, 1 + it * 4 + 2 * u + 2)
                    sp.dma_start(out[ds(it * 2 + u, 1)].rearrange("a (t p) d -> p (a t) d", p=P), ob[:, u]).then_inc(s_so[u], 16)
            for u in range(2):
                sp.wait_ge(s_so[u], 1 + 16 * (B // 2))

        @block.gpsimd
        def _(pool):
            for s in (s_y, s_vs):
                pool.sem_inc(s, 1)
            pool.memset(ident[:], 0.0).then_inc(s_zero, 1)
            pool.memset(ones[:], 1.0).then_inc(s_zero, 1)
            pool.memset(f2_z[:], 0.0).then_inc(s_zero, 1)
            pool.memset(fsum[:], 0.0).then_inc(s_zero, 1)
            pool.memset(fb2[:], 0.0).then_inc(s_zero, 1)
            pool.wait_ge(s_zero, 5)
            pool.affine_select(out=ident[:], in_=ident[:], compare_op=ALU.not_equal, fill=1.0, base=0,
                               pattern=[[-1, P]], channel_multiplier=1).then_inc(s_zero, 1)
            with pool.Fori(0, STEPS) as it:
                for g in range(ORDER * FJ):
                    base = it * (ORDER * FJ) + g
                    pool.wait_ge(s_xu, base + 1)
                    pool.wait_ge(s_yu, 1 + (base - 1 if g else it * (ORDER * FJ)))
                    m = prod[:, g % 2]
                    pool.tensor_tensor(spec[:, g % 2, 0], m[:, 0], m[:, 1], ALU.subtract)
                    pool.tensor_tensor(spec[:, g % 2, 1], m[:, 2], m[:, 3], ALU.add).then_inc(s_y, 1)
            pool.wait_ge(s_st2, STEPS)
            pool.memset(onesrow[:], 1.0).then_inc(s_one, 1)
            pool.memset(a_st[:], 1.0).then_inc(s_one, 1)
            pool.memset(q_z[:], 0.0).then_inc(s_one, 1)
            pool.dma_start(mask[:], c_mask).then_inc(s_ldm, 16)
            for u in range(2):
                pool.dma_start(m_mv[0:NPART * NT, u], c_chunk.rearrange("r (h t) -> r h t", h=NH)).then_inc(s_ldm, 16)
            pool.wait_ge(s_scr, 16 * N_SCR)
            pool.wait_ge(s_en, 2)
            pool.memset(cv[:, :, :, 0:NH, DH:V1], 1.0)
            pool.memset(cv[:, :, :, NH:NH + PADH], 0.0).then_inc(s_oned, 1)
            with pool.Fori(0, B // 2) as it:
                for u in range(2):
                    b = it * 2 + u
                    pool.wait_ge(s_cv, b + 1)
                    pool.wait_ge(s_sp, 1 + it * 4 + 2 * u)
                    for c in range(NT - 1):
                        i0 = c * (c + 1) // 2
                        w = en[:, i0:i0 + c + 1, ds(b * NH, NH)].unsqueeze(3).to_broadcast([P, c + 1, NH, V1])
                        last = pool.tensor_tensor(vs[:, i0:i0 + c + 1], cv[:, u, 0:c + 1, 0:NH], w, ALU.mult)
                    last.then_inc(s_vs, 1)
            pool.wait_ge(s_pv, 1 + B * NH)
            with pool.Fori(0, B // 2) as it:
                for u in range(2):
                    pool.wait_ge(s_ra, 1 + it * 2 + u + 1)
                    pool.wait_ge(s_ob, 1 + it * 4)
                    pool.tensor_tensor(rb[:, u], res[:, ds(it * (2 * NT) + u * NT, NT)],
                                       b2_bc[:].unsqueeze(1).to_broadcast([P, NT, D]), ALU.add).then_inc(s_rb, 1)

        @block.scalar
        def _(act):
            for s in (s_xt, s_gx, s_n0, s_fr):
                act.sem_inc(s, 1)
            act.wait_ge(s_feat, NT)
            act.activation(feat[:], feat[:], ACT.Silu).then_inc(s_silu, 1)

            def copy_out(job, dst, src):
                act.wait_ge(s_prep, job + 1)
                act.activation(dst, src, ACT.Copy).then_inc(s_prepc, 1)

            for i in range(WIN_JOBS):
                copy_out(i, win_t[:, :, 2 * P * i:2 * P * (i + 1)], bank[i][:].rearrange("p (k n) -> p k n", k=KT))
            copy_out(J_WOUT, wout_t[:], bank[J_WOUT % 8][:].rearrange("p (k n) -> p k n", k=KT))
            copy_out(J_GATE, wg_t[:], bank[J_GATE % 8][:, 0:6 * 2 * NH].rearrange("p (k n) -> p k n", k=6))
            act.wait_ge(s_prep, J_F2 + 1)
            act.wait_ge(s_zero, 5)
            act.activation(f2_z[0:HID, 0], bank[J_F2 % 8][0:HID, 0:D], ACT.Copy)
            act.activation(f2_z[HID:P, 1], bank[J_F2 % 8][HID:P, 0:D], ACT.Copy).then_inc(s_prepc, 1)
            for i, (c0, c1) in enumerate(FS_COLS):
                copy_out(J_FS + i, fs_t[:, c0:c1], bank[(J_FS + i) % 8][:, 0:c1 - c0])
            for n in range(NS):
                copy_out(J_H + n, filt[:, :, n, :], bank[(J_H + n) % 8][:].rearrange("p (o n) -> p o n", o=ORDER))
            for i in range(FT // 2):
                copy_out(J_W1 + i, wq1_t[:, :, 2 * P * i:2 * P * (i + 1)],
                         bank[(J_W1 + i) % 8][:].rearrange("p (k n) -> p k n", k=KT))
            for i in range(FT // 2):
                copy_out(J_W2 + i, wq2_t[:, 2 * i:2 * i + 2, :],
                         bank[(J_W2 + i) % 8][:].rearrange("p (k n) -> p k n", k=KT))
            act.wait_ge(s_quant, 2)

            def tokens(step, b):
                for k in range(KT):
                    q = b * KT + k
                    act.wait_ge(s_tp, 1 + step * 4 + q + 1)
                    act.wait_ge(s_hp, 1 + step * 4)
                    act.wait_ge(s_xf, 1 + step * 2)
                    act.activation(xn_t[:, k, b, 0:HALF], bank[q][:, 0:HALF], ACT.Copy)
                    act.activation(xn_t[:, k, b, HALF:L], bank[q][:, L - 1:HALF - 1:-1], ACT.Copy).then_inc(s_xt, 1)

            def copies_of(it, more=True):

                def gate2(q):
                    act.wait_ge(s_hp, 1 + it * 4 + q + 1)
                    act.wait_ge(s_v2, 1 + it * 4)
                    act.activation(g2_t[:, q // KT, q % KT], bank[q][:], ACT.Copy).then_inc(s_g2, 1)

                for q in range(4):
                    act.wait_ge(s_vp, 1 + it * 4 + q + 1)
                    act.wait_ge(s_x, 1 + it * (ORDER * FJ))
                    act.activation(vf[:, q // 2, q % 2], bank[4 + q][:], ACT.Copy).then_inc(s_vf, 1)
                for q in range(4):
                    act.wait_ge(s_gp, it * 4 + q + 1)
                    act.wait_ge(s_op, 1 + it * 4)
                    act.activation(g1[:, q // 2, q % 2], bank[q][:], ACT.Copy).then_inc(s_g1, 1)
                gate2(0)
                for nt in range(2):
                    act.wait_ge(s_yu, 1 + it * (ORDER * FJ) + FJ)
                    act.activation(even[:, nt], bank[4 + nt][:], ACT.Copy).then_inc(s_ev1, 1)
                for q in range(1, 4):
                    gate2(q)
                if more:
                    tokens(it + 1, 0)
                for q in range(4):
                    act.wait_ge(s_yu, 1 + it * (ORDER * FJ) + 2 * FJ)
                    act.wait_ge(s_u, it * 2 + 2)
                    act.activation(even_q[:, q], bank[4 + q][:, 0:HALF], ACT.Copy).then_inc(s_ev2, 1)
                if more:
                    tokens(it + 1, 1)

            for b in range(PB):
                tokens(0, b)
            with act.Fori(0, STEPS - 1) as it:
                copies_of(it)
            copies_of(STEPS - 1, more=False)
            act.activation(identb[:], ident[:], ACT.Copy).then_inc(s_idb, 1)
            with act.Fori(0, B // 2) as it:
                for u in range(2):
                    act.wait_ge(s_sq[u], 1 + it * 32)
                    act.wait_ge(s_gg, 1 + it * 2)
                    for q in range(4):
                        act.wait_ge(s_gt, 1 + it * 8 + 4 * u + q + 1)
                        dst = (q_t if q < KT else k_t)[:, u, q % KT]
                        act.activation(dst, bank[4 * u + q][:], ACT.Copy).then_inc(s_gx, 1)
            act.wait_ge(s_bg, 1)
            act.wait_ge(s_rows, 16)
            for i in range(2):
                act.activation(th[:, i], th[:, i], ACT.Tanh, bias=bg[:, i:i + 1], scale=1.0 / CAP).then_inc(s_tanh, 1)
            act.wait_ge(s_absf, 1)
            act.activation(sg[:, 1], sg[:, 0], ACT.Exp, scale=-1.0).then_inc(s_expf, 1)
            act.wait_ge(s_onep, 1)
            act.activation(sg[:, 3], sg[:, 2], ACT.Ln).then_inc(s_lnp, 1)
            act.wait_ge(s_mx, 1)
            for c in range(NT - 1):
                i0 = c * (c + 1) // 2
                act.activation(ek[:, i0:i0 + c + 1].rearrange("h c s -> h (c s)"), aw[:, 0:(c + 1) * P], ACT.Exp,
                               bias=nmx[:, (c + 1) * P - 1:(c + 1) * P])
            for c in range(1, NT):
                act.activation(ek[:, PAIRS + c - 1], mx[:, c * P:(c + 1) * P], ACT.Exp, scale=-1.0, bias=mx[:, c * P - 1:c * P])
            act.wait_ge(s_ms, 1)
            act.activation(ek[:, PAIRS + NT - 1:NEN].rearrange("h c s -> h (c s)"), msum[:], ACT.Exp, scale=-1.0).then_inc(s_ek, 1)
            for i, (n0, n1) in enumerate(((0, 8), (8, NEN))):
                act.wait_ge(s_ent, i + 1)
                act.activation(en[:, n0:n1], bank[2 + i][:, 0:(n1 - n0) * BH].rearrange("p (n r) -> p n r", r=BH), ACT.Copy).then_inc(s_en, 1)
            act.wait_ge(s_oned, 1)
            act.wait_ge(s_scr, 16 * N_SCR)

            def values(turn, u, first=False):
                act.wait_ge(s_bl[u], turn * (16 * N_BL) + 16 * N_BL)
                if not first:
                    act.wait_ge(s_pv, 1 + turn * (2 * NH) + u * NH - NH)
                act.activation(cv[:, u, :, 0:NH, 0:DH], ctx_s[:, u].rearrange("p t (h e) -> p t h e", h=NH), ACT.Copy).then_inc(s_cv, 1)

            def decays(turn, u, more=True):
                b = turn * 2 + u
                for h in range(NH):
                    n = turn * (2 * NH) + u * NH + h
                    act.wait_ge(s_sc, n + 1)
                    act.wait_ge(s_pm, 1 + (n - 1 if u * NH + h else n))
                    act.activation(edec[:, h % 2], bank[2 + h % 2][:], ACT.Exp).then_inc(s_ed, 1)
                    if h == NH // 2 and more:
                        values(turn + u, 1 - u)
                act.wait_ge(s_pv, 1 + b * NH + NH)
                act.wait_ge(s_ra, 1 + turn * 2)
                act.activation(num[:, u, 0], bank[4][:, 0:HV].rearrange("p (h e) -> p h e", h=NH), ACT.Copy).then_inc(s_n0, 1)
                act.wait_ge(s_num, 1 + b + 1)
                act.wait_ge(s_n0, 1 + b + 1)
                act.wait_ge(s_ra, 1 + b)
                act.activation(sq[:], num[:, u, :, :, 0:DH], ACT.Square).then_inc(s_sqr, 1)

            values(0, 0, first=True)
            with act.Fori(0, B // 2 - 1) as it:
                decays(it, 0)
                decays(it, 1)
            decays(B // 2 - 1, 0)
            decays(B // 2 - 1, 1, more=False)
            with act.Fori(0, B // 2) as it:

                def upper(u):
                    for k in range(KT):
                        act.wait_ge(s_xp, 1 + it * 4 + 2 * u + k + 1)
                        act.wait_ge(s_fo, 1 + it * (2 * FT))
                        act.activation(x3h[:, u, k], bank[k][:], ACT.Copy).then_inc(s_xh, 1)

                upper(0)
                for u in range(2):
                    for f in range(FT):
                        n = it * (2 * FT) + u * FT + f
                        if u == 0 and f == 1:
                            upper(1)
                        act.wait_ge(s_fp, n + 1)
                        act.wait_ge(s_fl, 1 + (n - 2 if u * FT + f > 1 else it * (2 * FT)))
                        act.activation(ff[:, f % 3], bank[2 + f % 4][:], ACT.Relu, bias=b1_col[:, f:f + 1]).then_inc(s_fr, 1)

        @block.tensor
        def _(pe):
            for s in (s_yu, s_hp, s_x, s_op, s_tp, s_vp, s_gt, s_gg, s_sp, s_pv, s_fo, s_xp):
                pe.sem_inc(s, 1)
            def begin(job):
                if job >= 8:
                    pe.wait_ge(s_prepc, copies(job - 8))
                return bank[job % 8]

            pe.wait_ge(s_zero, 6)
            pe.wait_ge(s_ldw, 16 * N_LDW)
            for i in range(WIN_JOBS):
                ps = begin(i)
                for k in range(KT):
                    for r in range(2):
                        last = pe.transpose(ps[:, (2 * k + r) * P:(2 * k + r + 1) * P],
                                            w_nat[:, 2 * i + r, k * P:(k + 1) * P], ident[:])
                last.then_inc(s_prep, 1)
            ps = begin(J_WOUT)
            for k in range(KT):
                for r in range(KT):
                    last = pe.transpose(ps[:, (2 * k + r) * P:(2 * k + r + 1) * P], wo_nat[:, r, k * P:(k + 1) * P], ident[:])
            last.then_inc(s_prep, 1)
            ps = begin(J_GATE)
            for k in range(6):
                last = pe.transpose(ps[:, k * 2 * NH:(k + 1) * 2 * NH], g_nat[:, k * P:(k + 1) * P],
                                    ident[0:2 * NH, 0:2 * NH])
            last.then_inc(s_prep, 1)
            ps = begin(J_F2)
            pe.wait_ge(s_ldf, 16 * N_LDF)
            for k in range(KT):
                last = pe.transpose(ps[:, k * P:(k + 1) * P], f2_nat[:, k].rearrange("p o h -> p (o h)"), ident[:])
            last.then_inc(s_prep, 1)
            pe.wait_ge(s_silu, 1)
            for i, (c0, c1) in enumerate(FS_COLS):
                ps = begin(J_FS + i)
                for t in range(NT):
                    last = pe.matmul(ps[:, 0:c1 - c0], feat[:, t], h_fwd[:, t, c0:c1], start=(t == 0), stop=(t == NT - 1))
                last.then_inc(s_prep, 1)
            pe.wait_ge(s_prepc, copies(J_FS + len(FS_COLS) - 1))
            for n in range(NS):
                ps = begin(J_H + n)
                for o in range(ORDER):
                    half = ps[:, o * D:(o + 1) * D]
                    pe.matmul(half, fs_t[:, n * P:(n + 1) * P], f2_z[:, o], start=True, stop=False)
                    last = pe.matmul(half, fsum[:, n * P:(n + 1) * P], fb2[:, o], start=False, stop=True)
                last.then_inc(s_prep, 1)
            ps = begin(J_SUM)
            pe.wait_ge(s_qabs, 2)
            pe.matmul(ps[:, 0:2], ones[:], qsum[:], start=True, stop=True).then_inc(s_prep, 1)
            for i in range(FT // 2):
                ps = begin(J_W1 + i)
                pe.wait_ge(s_quant, 1)
                for k in range(KT):
                    for r in range(2):
                        last = pe.transpose(ps[:, (2 * k + r) * P:(2 * k + r + 1) * P],
                                            w1_nat[:, 2 * i + r, k * P:(k + 1) * P], ident[:])
                last.then_inc(s_prep, 1)
            for i in range(FT // 2):
                ps = begin(J_W2 + i)
                pe.wait_ge(s_quant, 2)
                for r in range(2):
                    for k in range(KT):
                        last = pe.transpose(ps[:, (2 * r + k) * P:(2 * r + k + 1) * P],
                                            w2_nat[:, k, (2 * i + r) * P:(2 * i + r + 1) * P], ident[:])
                last.then_inc(s_prep, 1)
            pe.wait_ge(s_prepc, copies(JOBS - 1))
            pe.wait_ge(s_ldt, 32)

            def transposes(step, b):
                pe.wait_ge(s_xn, step * (PB * NT) + (b + 1) * NT)
                for k in range(KT):
                    for t in range(NT):
                        last = pe.transpose(bank[b * KT + k][:, t * P:(t + 1) * P], xn[:, b * NT + t, k * P:(k + 1) * P],
                                            ident[:])
                    last.then_inc(s_tp, 1)

            def convolutions(it, more=True):
                tile0 = it * (ORDER * FJ)

                pe.wait_ge(s_xf, 1 + it * 2 + 2)
                pe.wait_ge(s_v2, 1 + it * 4)
                for q in range(4):
                    pm, nt = q // 2, q % 2
                    for b in range(PB):
                        for k in range(KT):
                            last = pe.matmul(bank[4 + q][:, b * D:(b + 1) * D], xf[:, pm, k, b, nt * P:(nt + 1) * P],
                                             win_t[:, k, 0:D], start=(k == 0), stop=(k == KT - 1))
                    last.then_inc(s_vp, 1)
                pe.wait_ge(s_xt, 1 + it * 4 + 4)
                pe.wait_ge(s_res, 1 + it * 4)
                for q in range(4):
                    back, nt = q // 2, q % 2
                    for b in range(PB):
                        for k in range(KT):
                            t0 = back * HALF + nt * P
                            last = pe.matmul(bank[q][:, b * D:(b + 1) * D],
                                             xn_t[:, k, b, t0:t0 + P],
                                             win_t[:, k, D:2 * D], start=(k == 0), stop=(k == KT - 1))
                    last.then_inc(s_gp, 1)

                def gate2(q):
                    b, dh = q // KT, q % KT
                    pe.wait_ge(s_xu, tile0 + 3 + q // 2)
                    for k in range(KT):
                        last = pe.matmul(bank[q][:], win_t[:, k, 2 * D + dh * P:2 * D + (dh + 1) * P],
                                         xn_t[:, k, b], start=(k == 0), stop=(k == KT - 1))
                    last.then_inc(s_hp, 1)

                def forward(o, j):
                    g = o * FJ + j
                    if g >= 2:
                        pe.wait_ge(s_xu, tile0 + g - 1)
                    is_even = j < FJ // 2
                    for cs in range(2):
                        pm = cs if is_even else 1 - cs
                        for nt in range(2):
                            last = pe.matmul(bank[2 * (g % 2) + cs][:], fwd[:, nt, j, cs], vf[:, pm, nt],
                                             start=(nt == 0), stop=(nt == 1))
                    last.then_inc(s_x, 1)

                def part(j, cs):
                    return cs if j < FJ // 2 else 1 - cs

                def backward1(j):
                    pe.wait_ge(s_y, 1 + tile0 + j + 1)
                    for cs in range(2):
                        for nt in range(2):
                            last = pe.matmul(bank[4 + 2 * part(j, cs) + nt][:], inv[:, j, cs, nt * P:(nt + 1) * P],
                                             spec[:, j % 2, cs], start=(j == 0), stop=(j == FJ - 1))
                    last.then_inc(s_yu, 1)

                def backward2(j):
                    pe.wait_ge(s_y, 1 + tile0 + FJ + j + 1)
                    for cs in range(2):
                        odd = part(j, cs)
                        for q in range(4):
                            last = pe.matmul(bank[4 + q][:, odd * HALF:(odd + 1) * HALF],
                                             spec[:, j % 2, cs, q * P:(q + 1) * P], inv[:, j, cs],
                                             start=(j == 0 and cs == 0), stop=(j == FJ - 1), skip_group_check=True)
                    last.then_inc(s_yu, 1)

                pe.wait_ge(s_g1, it * 4 + 4)
                pe.wait_ge(s_vf, it * 4 + 4)
                forward(0, 0)
                forward(0, 1)
                for j in range(FJ):
                    if j == FJ - 1:
                        gate2(0)
                    backward1(j)
                    if j + 2 < FJ:
                        forward(0, j + 2)
                for q in range(1, 4):
                    gate2(q)
                pe.wait_ge(s_v1, it * 2 + 2)
                pe.wait_ge(s_g2, it * 4 + 4)
                forward(1, 0)
                forward(1, 1)
                pe.wait_ge(s_ev1, it * 2 + 2)
                pe.wait_ge(s_u, it * 2 + 2)
                for j in range(FJ):
                    if j == FJ - 1 and more:
                        pe.wait_ge(s_xu, tile0 + ORDER * FJ - 1)
                        transposes(it + 1, 0)
                    backward2(j)
                    if j + 2 < FJ:
                        forward(1, j + 2)
                pe.wait_ge(s_xu, tile0 + ORDER * FJ)
                if more:
                    transposes(it + 1, 1)
                for q in range(4):
                    b = q // 2
                    if more:
                        pe.wait_ge(s_xt, 1 + it * 4 + 4 + q + 1)
                    pe.wait_ge(s_v2, 1 + it * 4 + 2 * b + 2)
                    for r in range(2):
                        t = 2 * (q % 2) + r
                        for k in range(KT):
                            last = pe.matmul(bank[q][:, r * D:(r + 1) * D], v2_t[:, b, k, t * P:(t + 1) * P],
                                             wout_t[:, k], start=(k == 0), stop=(k == KT - 1))
                    last.then_inc(s_op, 1)

            for b in range(PB):
                transposes(0, b)
            with pe.Fori(0, STEPS - 1) as it:
                convolutions(it)
            convolutions(STEPS - 1, more=False)
            with pe.Fori(0, B // 2) as it:
                for u in range(2):
                    pe.wait_ge(s_gv, 1 + it * 2)
                    pe.wait_ge(s_gx, 1 + it * 8)
                    pe.wait_ge(s_qn, it * 2 + u + 1)
                    for q in range(2 * KT):
                        if q == KT:
                            pe.wait_ge(s_cl[u], it * 16 + 16)
                        src = (qn if q < KT else ctx_s)[:, u]
                        k = q % KT
                        for t in range(NT):
                            last = pe.transpose(bank[4 * u + q][:, t * P:(t + 1) * P], src[:, t, k * P:(k + 1) * P], ident[:])
                        last.then_inc(s_gt, 1)
                for u in range(2):
                    pe.wait_ge(s_gx, 1 + it * 8 + 4 * u + 4)
                    pe.wait_ge(s_wkv, 1)
                    for q in range(2 * KT):
                        k = q % KT
                        src, w = (q_t, wg_t) if q < KT else (k_t, wkv)
                        last = pe.matmul(bank[4 * u][0:2 * NH, :], w[:, k], src[:, u, k], start=(q == 0), stop=(q == 2 * KT - 1))
                    last.then_inc(s_gg, 1)
            pe.wait_ge(s_ek, 1)
            for i, (n0, n1) in enumerate(((0, 8), (8, NEN))):
                for n in range(n0, n1):
                    last = pe.transpose(bank[2 + i][:, (n - n0) * BH:(n - n0 + 1) * BH], ek[:, n], ident[0:BH, 0:BH])
                last.then_inc(s_ent, 1)
            pe.wait_ge(s_en, 2)
            pe.wait_ge(s_idb, 1)
            pe.wait_ge(s_ldm, 48)
            with pe.Fori(0, B // 2) as it:
                for u in range(2):
                    b = it * 2 + u

                    def scores(h):
                        n = it * (2 * NH) + u * NH + h
                        k = h // HT
                        pe.wait_ge(s_pm, 1 + (n - 1 if u * NH + h else n))
                        for c in range(NT):
                            t = slice(c * P, (c + 1) * P)
                            pe.matmul(bank[h % 2][:, t], k_t[:, u, k, t], q_z[:, u, h % HT, k, t], start=True, stop=True)
                        pe.matmul(bank[2 + h % 2][:], identb[:], mask[:], start=True, stop=False)
                        pe.matmul(bank[2 + h % 2][:], a_st[:, u, h], m_mv[:, u, h], start=False, stop=True).then_inc(s_sc, 1)

                    pe.wait_ge(s_bl[u], it * (16 * N_BL) + 16 * N_BL)
                    scores(0)
                    scores(1)
                    pe.wait_ge(s_vs, 1 + b + 1)
                    pe.wait_ge(s_num, 1 + b)
                    pe.wait_ge(s_n0, 1 + b)
                    for k in range(KT):
                        for c in range(NT - 1):
                            for j in range(c + 1):
                                last = pe.matmul(bank[4 + k][:, c * GV:(c + 1) * GV], ctx_s[:, u, j, k * P:(k + 1) * P],
                                                 vs[:, c * (c + 1) // 2 + j].rearrange("p h e -> p (h e)")[:, k * GV:(k + 1) * GV],
                                                 start=(j == 0), stop=(j == c))
                        last.then_inc(s_sp, 1)
                    for k in range(KT):
                        pe.wait_ge(s_bd, b * 2 + k + 1)
                        for c in (2, 3, 1) if k == 0 else (1, 2, 3):
                            if k == 0 and c == 1:
                                pe.wait_ge(s_bd, b * 2 + 2)
                            last = pe.matmul(bank[4 + c][:, k * GV:(k + 1) * GV], q_t[:, u, k, c * P:(c + 1) * P], bd[:, k, c - 1],
                                             start=True, stop=True)
                            if k == KT - 1:
                                last.then_inc(s_ip, 1)
                    for h in range(NH):
                        pe.wait_ge(s_pm, 1 + it * (2 * NH) + u * NH + h + 1)
                        for c in range(NT):
                            if h == 0 and c > 0:
                                pe.wait_ge(s_in, b * (NT - 1) + c)
                            last = pe.matmul(bank[4 + c][:, h * V1:(h + 1 + PADH) * V1], pmat[:, h % 2, c * P:(c + 1) * P],
                                             cv[:, u, c, h:h + 1 + PADH].rearrange("p h e -> p (h e)"), start=True, stop=True)
                        last.then_inc(s_pv, 1)
                        if h + 2 < NH:
                            scores(h + 2)
            with pe.Fori(0, B // 2) as it:

                def turn(u):
                    pe.wait_ge(s_x3, it * 2 + u + 1)
                    pe.wait_ge(s_xl, 1 + it * 4 + 2 * u)
                    for k in range(KT):
                        for t in range(NT):
                            last = pe.transpose(bank[k][:, t * P:(t + 1) * P], x3[:, u, t, k * P:(k + 1) * P], ident[:])
                        last.then_inc(s_xp, 1)

                def hidden(u, f):
                    n = it * (2 * FT) + u * FT + f
                    pe.wait_ge(s_fr, 1 + (n - 3 if u * FT + f > 2 else it * (2 * FT)))
                    for k in range(KT):
                        for i, part_ in enumerate((x3h, x3l)):
                            last = pe.matmul(bank[2 + f % 4][:], wq1_t[:, k, f * P:(f + 1) * P], part_[:, u, k],
                                             start=(k == 0 and i == 0), stop=(k == KT - 1 and i == 1))
                    last.then_inc(s_fp, 1)

                turn(0)
                for u in range(2):
                    pe.wait_ge(s_xl, 1 + it * 4 + 2 * u + 2)
                    hidden(u, 0)
                    hidden(u, 1)
                    if u == 0:
                        turn(1)
                    pe.wait_ge(s_ob, 1 + it * 4 + 2 * u)
                    for f in range(FT):
                        if f + 2 < FT:
                            hidden(u, f + 2)
                        n = it * (2 * FT) + u * FT + f
                        for i, part_ in enumerate((ffh, ffl)):
                            if i == 0:
                                pe.wait_ge(s_fh, n + 1)
                            else:
                                pe.wait_ge(s_fl, 1 + n + 1)
                            for t in range(NT):
                                last = pe.matmul(bank[6 + t // 2][:, (t % 2) * D:(t % 2 + 1) * D], part_[:, f % 4, t * P:(t + 1) * P],
                                                 wq2_t[:, f], start=(f == 0 and i == 0 and t % 2 == 0),
                                                 stop=(f == FT - 1 and i == 1), skip_group_check=True)
                        last.then_inc(s_fo, 1)

        @block.vector
        def _(dve):
            for s in (s_xf, s_v2, s_res, s_gv, s_pm, s_ra, s_num, s_ob, s_fl, s_xl):
                dve.sem_inc(s, 1)
            def token_roots(own, t0, t1):
                for i in range(t0, t1):
                    last = dve.bn_aggr(mv[:, i], stats[:, i])
                own.then(last)
                own.then(dve.tensor_scalar(var_eps[:, t0:t1], mv[:, t0:t1, 1], LN_EPS, None, ALU.add))
                inverse_root(own, dve, rstd[:, t0:t1], var_eps[:, t0:t1], nwt[:, t0:t1])

            own = Count(dve, own_p)
            dve.wait_ge(s_ldf, 16 * N_LDF)
            for t in range(NT):
                dve.scalar_tensor_tensor(feat[:, t], fw1_bc[:], time[:, t:t + 1], fb1_bc[:], ALU.mult, ALU.add).then_inc(s_feat, 1)
            dve.wait_ge(s_ldx, 16 * B)
            for i in range(TILES):
                last = dve.bn_stats(stats[:, i], res[:, i])
            own.then(last)
            for i in range(TILES):
                last = dve.bn_aggr(mv[:, i], stats[:, i])
            own.then(last)
            own.then(dve.tensor_scalar(var_eps[:], mv[:, :, 1], LN_EPS, None, ALU.add))
            inverse_root(own, dve, rstd[:], var_eps[:], nwt[:])
            dve.wait_ge(s_ldq, 16 * N_LDQ)
            w1_flat = w1_nat[:].rearrange("p i c -> p (i c)")
            w2_flat = w2_nat[:].rearrange("p i c -> p (i c)")
            for i, flat in enumerate((w1_flat, w2_flat)):
                dve.tensor_reduce(qsum[:, i:i + 1], flat, AX_X, ALU.add, apply_absolute_value=True).then_inc(s_qabs, 1)
            own.then(dve.tensor_scalar(gain[:], gain[:], 1.0, None, ALU.add))
            dve.wait_ge(s_prep, J_SUM + 1)
            own.then(dve.tensor_scalar(qden[:], bank[J_SUM % 8][:, 0:2], 1.0 / (FF * D), Q_EPS, ALU.mult, ALU.add))
            own.then(dve.reciprocal(qrec[:], qden[:]))
            for i, flat in enumerate((w1_flat, w2_flat)):
                own.then(dve.tensor_scalar(flat, flat, qrec[:, i:i + 1], 1.0, ALU.mult, ALU.min))
                own.then(dve.tensor_scalar(flat, flat, -1.0, ROUND, ALU.max, ALU.add))
                dve.tensor_scalar(flat, flat, -ROUND, None, ALU.add).then_inc(s_quant, 1)
            dve.wait_ge(s_prep, JOBS)
            dve.wait_ge(s_prepc, copies(JOBS - 1))

            own = Count(dve, own_a)
            own_roots_a = Count(dve, own_n)
            OWN_A = 2

            def normalise(step, b):
                dve.wait_ge(s_tp, 1 + step * 4)
                for i in range(b * NT, (b + 1) * NT):
                    one = ds(step * (PB * NT) + i, 1)
                    dve.tensor_scalar(xn[:, i:i + 1], res[:, one], mv[:, one, 0], rstd[:, one],
                                      ALU.subtract, ALU.mult).then_inc(s_xn, 1)

            def fold(step):
                dve.wait_ge(s_xt, 1 + step * 4 + 4)
                dve.wait_ge(s_vp, 1 + step * 4)
                for pm, op in enumerate((ALU.add, ALU.subtract)):
                    dve.tensor_tensor(xf[:, pm], xn_t[:, :, :, 0:HALF], xn_t[:, :, :, HALF:L], op).then_inc(s_xf, 1)

            def gating(it, more=True):
                own.from_(it * OWN_A)

                def products(o, j):
                    g = o * FJ + j
                    tile = it * (ORDER * FJ) + g
                    dve.wait_ge(s_x, 1 + tile + 1)
                    dve.wait_ge(s_y, 1 + (tile - 1 if g else it * (ORDER * FJ)))
                    xc, xs = (bank[2 * (g % 2) + cs][:].rearrange("p (b d) -> p b d", b=PB) for cs in range(2))
                    h = [filt[:, o, n].unsqueeze(1).to_broadcast([P, PB, D]) for n in (j, FJ + j, 2 * FJ if j == 0 else j)]
                    for i, (spectrum, filter_) in enumerate(((xc, h[0]), (xs, h[1]), (xs, h[2]), (xc, h[1]))):
                        last = dve.tensor_tensor(prod[:, g % 2, i].rearrange("p (b d) -> p b d", b=PB), spectrum,
                                                 filter_, ALU.mult)
                    last.then_inc(s_xu, 1)

                for j in range(FJ):
                    products(0, j)
                dve.wait_ge(s_x, 1 + it * (ORDER * FJ) + FJ)
                for nt in range(2):
                    dve.wait_ge(s_ev1, it * 2 + nt + 1)
                    odd = bank[6 + nt][:]
                    dve.tensor_tensor(ysum[:, nt, 0], even[:, nt], odd, ALU.add)
                    dve.tensor_tensor(ysum[:, nt, 1], even[:, nt], odd, ALU.subtract).then_inc(s_u, 1)
                for nt in range(2):
                    dve.wait_ge(s_u, it * 2 + nt + 1)
                    dve.tensor_tensor(ysum[:, nt, 0], ysum[:, nt, 0], g1[:, 0, nt], ALU.mult)
                    own.then(dve.tensor_tensor(ysum[:, nt, 1], ysum[:, nt, 1], g1[:, 1, nt], ALU.mult))
                    dve.tensor_tensor(vf[:, 0, nt], ysum[:, nt, 0], ysum[:, nt, 1], ALU.add)
                    dve.tensor_tensor(vf[:, 1, nt], ysum[:, nt, 0], ysum[:, nt, 1], ALU.subtract).then_inc(s_v1, 1)
                for j in range(FJ):
                    products(1, j)
                    if j < PB and more:
                        normalise(it + 1, j)
                    if j == 1 and not more:
                        dve.wait_ge(s_st2, STEPS - 1)
                        token_roots(own_roots_a, 0, (STEPS - 1) * PB * NT)
                for q in range(4):
                    dve.wait_ge(s_ev2, it * 4 + q + 1)
                    odd = bank[4 + q][:, HALF:L]
                    dve.tensor_tensor(ysum_q[:, q, 0], even_q[:, q], odd, ALU.add)
                    dve.tensor_tensor(ysum_q[:, q, 1], even_q[:, q], odd, ALU.subtract).then_inc(s_u2, 1)
                for q in range(4):
                    b, dh = q // KT, q % KT
                    dve.wait_ge(s_u2, it * 4 + q + 1)
                    dve.tensor_tensor(v2_t[:, b, dh, 0:HALF], ysum_q[:, q, 0], g2_t[:, b, dh, 0:HALF], ALU.mult)
                    dve.tensor_tensor(v2_t[:, b, dh, L - 1:HALF - 1:-1], ysum_q[:, q, 1],
                                      g2_t[:, b, dh, HALF:L], ALU.mult).then_inc(s_v2, 1)
                if more:
                    fold(it + 1)
                for q in range(4):
                    two = ds(it * (PB * NT) + 2 * q, 2)
                    dve.wait_ge(s_op, 1 + it * 4 + q + 1)
                    dve.tensor_tensor(res[:, two], res[:, two], bank[q][:].rearrange("p (t d) -> p t d", t=2),
                                      ALU.add).then_inc(s_res, 1)
                for q in range(4):
                    dve.wait_ge(s_res, 1 + it * 4 + q + 1)
                    for r in range(2):
                        one = ds(it * (PB * NT) + 2 * q + r, 1)
                        last = dve.bn_stats(stats[:, one], res[:, one])
                last.then_inc(s_st2, 1)
                assert own.n == OWN_A

            for b in range(PB):
                normalise(0, b)
            fold(0)
            with dve.Fori(0, STEPS - 1) as it:
                gating(it)
            gating(STEPS - 1, more=False)
            def tokens2(turn, u):
                dve.wait_ge(s_gt, 1 + turn * 8)
                for t in range(NT):
                    one = ds(turn * (2 * NT) + u * NT + t, 1)
                    last = dve.tensor_scalar(qn[:, u, t:t + 1], res[:, one], mv[:, one, 0], rstd[:, one], ALU.subtract, ALU.mult)
                last.then_inc(s_qn, 1)

            def gates(it, more=True):
                for u in range(2):
                    if more:
                        tokens2(it + 1, u)
                for u in range(2):
                    dve.wait_ge(s_gg, 1 + it * 2 + u + 1)
                    dve.wait_ge(s_sg[u], 1 + it * 32)
                    dve.tensor_copy(rows[:, u], bank[4 * u][0:2 * NH, :]).then_inc(s_gv, 1)

            own = own_roots_a
            dve.wait_ge(s_st2, STEPS)
            tokens2(0, 0)
            tokens2(0, 1)
            dve.tensor_tensor(wkv[:], wg_t[:, KT:2 * KT], wg_t[:, 2 * KT:3 * KT], ALU.add).then_inc(s_wkv, 1)
            token_roots(own, (STEPS - 1) * PB * NT, TILES)
            with dve.Fori(0, B // 2 - 1) as it:
                gates(it)
            gates(B // 2 - 1, more=False)

            own = Count(dve, own_s)
            dve.wait_ge(s_bgl, 16 * 2 * B)
            dve.tensor_scalar(bg[:], bg[:], 1.0 / CAP, None, ALU.mult).then_inc(s_bg, 1)
            dve.wait_ge(s_tanh, 2)
            own.then(dve.tensor_scalar(th[:], th[:], CAP, None, ALU.mult))
            dve.scalar_tensor_tensor(sg[:, 0], th[:, 1], -1.0, th[:, 1], ALU.mult, ALU.max).then_inc(s_absf, 1)
            dve.wait_ge(s_expf, 1)
            dve.tensor_scalar(sg[:, 2], sg[:, 1], 1.0, None, ALU.add).then_inc(s_onep, 1)
            dve.wait_ge(s_onep, 1)
            own.then(dve.tensor_scalar(sg[:, 4], sg[:, 2], -1.0, None, ALU.add))
            own.then(dve.tensor_scalar(sg[:, 5], sg[:, 4], 1e-10, None, ALU.max))
            own.then(dve.reciprocal(sg[:, 5], sg[:, 5]))
            own.then(dve.tensor_scalar(sg[:, 4], sg[:, 4], 0.0, None, ALU.is_equal))
            dve.wait_ge(s_lnp, 1)
            own.then(dve.tensor_tensor(sg[:, 3], sg[:, 3], sg[:, 5], ALU.mult))
            own.then(dve.tensor_tensor(sg[:, 3], sg[:, 3], sg[:, 4], ALU.add))
            own.then(dve.tensor_tensor(sg[:, 3], sg[:, 3], sg[:, 1], ALU.mult))
            own.then(dve.scalar_tensor_tensor(sg[:, 0], th[:, 1], 0.0, sg[:, 3], ALU.min, ALU.subtract))
            dve.wait_ge(s_one, 1)
            own.then(dve.tensor_tensor_scan(lf[:], onesrow[:], sg[:, 0], 0.0, ALU.mult, ALU.add))
            own.then(dve.tensor_tensor(aw[:], th[:, 0], lf[:], ALU.subtract))
            own.then(dve.tensor_tensor_scan(mx[:], aw[:], aw[:], -3e38, ALU.max, ALU.max))
            dve.tensor_scalar(nmx[:], mx[:], -1.0, None, ALU.mult).then_inc(s_mx, 1)
            dve.tensor_tensor(msum[:], lf[:], mx[:], ALU.add).then_inc(s_ms, 1)
            dve.wait_ge(s_mx, 1)
            for parts, whole, r in ((ap3, aw, 0), (mp3, nmx, 2)):
                own.then(dve.tensor_copy(parts[:, 0], whole[:]))
                own.then(dve.tensor_tensor(rem[:, r], whole[:], parts[:, 0], ALU.subtract))
                own.then(dve.tensor_copy(parts[:, 1], rem[:, r]))
                own.then(dve.tensor_tensor(rem[:, r + 1], rem[:, r], parts[:, 1], ALU.subtract))
                dve.tensor_copy(parts[:, 2], rem[:, r + 1]).then_inc(s_parts, 1)

            own = Count(dve, own_b)
            OWN_B = 21
            FINISH = 8
            dve.wait_ge(s_en, 2)
            dve.wait_ge(s_scr, 16 * N_SCR)
            dve.wait_ge(s_lda, 16)

            def finish(b, u, step):
                row = ds(b * NH, NH)
                total = num[:, u, :, :, DH]
                den, rden, ms, v, tmp, f = (tiny[:, i] for i in range(6))
                flat = hout[:].rearrange("p t h e -> p t (h e)")
                if step == 0:
                    own.from_(b * OWN_B)
                    own.then(dve.scalar_tensor_tensor(den, total, -1.0, total, ALU.mult, ALU.max))
                    own.then(dve.tensor_tensor(den, den, en[:, PAIRS + NT - 1:NEN, row], ALU.max))
                    own.then(dve.tensor_scalar(den, den, DEN_EPS, None, ALU.add))
                    own.then(dve.reciprocal(rden, den))
                elif step == 1:
                    dve.wait_ge(s_sqr, b + 1)
                    own.then(dve.tensor_reduce(ms, sq[:], AX_X, ALU.add))
                elif step == 2:
                    own.then(dve.tensor_tensor(ms, ms, rden, ALU.mult))
                    own.then(dve.tensor_tensor(ms, ms, rden, ALU.mult))
                    own.then(dve.tensor_scalar(v, ms, 1.0 / DH, RMS_EPS, ALU.mult, ALU.add))
                    root_guess(own, dve, f, v)
                elif step == 3:
                    root_step(own, dve, f, v, tmp)
                    root_step(own, dve, f, v, tmp)
                elif step == 4:
                    root_step(own, dve, f, v, tmp)
                    own.then(dve.tensor_tensor(f, f, rden, ALU.mult))
                elif step == 5:
                    own.then(dve.tensor_tensor(hout[:], num[:, u, :, :, 0:DH], f.unsqueeze(3).to_broadcast([P, NT, NH, DH]), ALU.mult))
                elif step == 6:
                    own.then(dve.tensor_tensor(flat, flat, gain[:].unsqueeze(1).to_broadcast([P, NT, D]), ALU.mult))
                    assert own.n == OWN_B
                else:
                    dve.tensor_tensor(res[:, ds(b * NT, NT)], res[:, ds(b * NT, NT)], flat, ALU.add).then_inc(s_ra, 1)

            def token_stats(b):
                dve.wait_ge(s_ra, 1 + b + 1)
                for t in range(NT):
                    last = dve.bn_stats(stats[:, ds(b * NT + t, 1)], res[:, ds(b * NT + t, 1)])
                last.then_inc(s_st3, 1)

            def batch(turn, u, before=None):
                b = turn * 2 + u
                row = ds(b * NH, NH)
                for k in range(KT):
                    dve.wait_ge(s_sp, 1 + b * 2 + k + 1)
                    dve.tensor_tensor(bd[:, k], bank[4 + k][:, 0:(NT - 1) * GV].rearrange("p (c e) -> p c e", c=NT - 1),
                                      heads[:].unsqueeze(1).to_broadcast([P, NT - 1, GV]), ALU.mult).then_inc(s_bd, 1)
                for c in range(1, NT):
                    dve.wait_ge(s_ip, b * (NT - 1) + c)
                    w = en[:, PAIRS + c - 1, row].unsqueeze(2).to_broadcast([P, NH, V1])
                    dve.tensor_tensor(inter[:, c - 1], bank[4 + c][:, 0:HV].rearrange("p (h e) -> p h e", h=NH), w,
                                      ALU.mult).then_inc(s_in, 1)
                for h in range(NH):
                    n = turn * (2 * NH) + u * NH + h
                    dve.wait_ge(s_ed, n + 1)
                    dve.wait_ge(s_pv, 1 + (n - 1 if u * NH + h else n))
                    dve.scalar_tensor_tensor(pmat[:, h % 2], bank[h % 2][:], float(DH) ** -0.5, edec[:, h % 2], ALU.mult,
                                             ALU.mult).then_inc(s_pm, 1)
                    if before is not None:
                        finish(before, 1 - u, h)
                dve.wait_ge(s_pv, 1 + b * NH + NH)
                dve.wait_ge(s_in, b * (NT - 1) + NT - 1)
                for c in range(1, NT):
                    last = dve.tensor_tensor(num[:, u, c], bank[4 + c][:, 0:HV].rearrange("p (h e) -> p h e", h=NH),
                                             inter[:, c - 1], ALU.add)
                last.then_inc(s_num, 1)
                if before is not None:
                    token_stats(before)
                dve.wait_ge(s_num, 1 + b + 1)
                dve.wait_ge(s_n0, 1 + b + 1)

            batch(0, 0)
            with dve.Fori(0, B // 2 - 1) as it:
                batch(it, 1, it * 2)
                batch(it + 1, 0, it * 2 + 1)
            own_roots = Count(dve, own_f)
            dve.wait_ge(s_st3, 2)
            token_roots(own_roots, 0, 2 * NT)
            batch(B // 2 - 1, 1, B - 2)

            def tokens3(turn, u):
                dve.wait_ge(s_xp, 1 + turn * 4)
                for t in range(NT):
                    one = ds(turn * (2 * NT) + u * NT + t, 1)
                    last = dve.tensor_scalar(x3[:, u, t:t + 1], res[:, one], mv[:, one, 0], rstd[:, one], ALU.subtract, ALU.mult)
                last.then_inc(s_x3, 1)

            tokens3(0, 0)
            tokens3(0, 1)
            def feed_forward(it, first=False, more=True):

                def lower(u):
                    for k in range(KT):
                        dve.wait_ge(s_xh, it * 4 + 2 * u + k + 1)
                        dve.wait_ge(s_fo, 1 + it * (2 * FT))
                        dve.tensor_tensor(x3l[:, u, k], bank[k][:], x3h[:, u, k].bitcast(F32), ALU.subtract).then_inc(s_xl, 1)

                lower(0)
                for u in range(2):
                    for f in range(FT):
                        n = it * (2 * FT) + u * FT + f
                        if u == 0 and f == 1:
                            lower(1)
                        if u == 1 and 2 <= f < 4 and more:
                            tokens3(it + 1, f - 2)
                        dve.wait_ge(s_fr, 1 + n + 1)
                        dve.wait_ge(s_fo, 1 + (n - 3 if u * FT + f > 2 else it * (2 * FT)))
                        dve.tensor_copy(ffh[:, f % 4], ff[:, f % 3]).then_inc(s_fh, 1)
                        dve.wait_ge(s_fh, n + 1)
                        dve.tensor_tensor(ffl[:, f % 4], ff[:, f % 3], ffh[:, f % 4].bitcast(F32), ALU.subtract).then_inc(s_fl, 1)
                        if first and u == 0:
                            finish(B - 1, 1, f)
                        elif first and f == 0:
                            token_stats(B - 1)
                        elif first and f == 1:
                            dve.wait_ge(s_st3, B)
                            token_roots(own_roots, 2 * NT, TILES)
                    dve.wait_ge(s_fo, 1 + it * (2 * FT) + (u + 1) * FT)
                    dve.wait_ge(s_rb, it * 2 + u + 1)
                    dve.wait_ge(s_so[u], 1 + it * 16)
                    for i in range(2):
                        dve.tensor_tensor(ob[:, u, 2 * i:2 * i + 2], rb[:, u, 2 * i:2 * i + 2],
                                          bank[6 + i][:].rearrange("p (t d) -> p t d", t=2), ALU.add).then_inc(s_ob, 1)

            assert FINISH <= FT
            feed_forward(0, first=True)
            with dve.Fori(1, B // 2 - 1) as it:
                feed_forward(it)
            feed_forward(B // 2 - 1, more=False)


_INS = ['x', 'ctx_1024', 'L0_attn_W_in', 'L0_attn_W_out', 'L0_attn_f_w1', 'L0_attn_f_b1', 'L0_attn_f_w2',
        'L0_attn_f_b2', 'L0_xattn_ifgate_w', 'L0_xattn_ifgate_b', 'L0_xattn_outnorm_w', 'L0_ffn_W1', 'L0_ffn_b1',
        'L0_ffn_W2', 'L0_ffn_b2']


def kernel(**inputs):
    import concourse.bacc as bacc
    from concourse.bass_utils import run_bass_kernel_spmd

    nc = bacc.Bacc("TRN2", target_bir_lowering=False, num_devices=1)
    arrays = {f"in_{name}_dram": np.ascontiguousarray(inputs[name]) for name in _INS}
    for name, table in tables().items():
        arrays[f"table_{name}_dram"] = table
    args = [nc.dram_tensor(name, a.shape, mybir.dt.from_np(a.dtype), kind="ExternalInput").ap()
            for name, a in arrays.items()]
    args.append(nc.dram_tensor("out_0_dram", (B, L, D), F32, kind="ExternalOutput").ap())
    decoder_layer(nc, *args)
    r = run_bass_kernel_spmd(nc, [arrays], core_ids=[0])
    return r.results[0]["out_0_dram"]
```
